# Optimizing a Trainium2 kernel written in Bass

```python
import numpy as np
import jax
import jax.numpy as jnp

def _softmax(x, axis=-1):
    return jax.nn.softmax(x, axis=axis)

def _gelu(x):
    return jax.nn.gelu(x, approximate=True)

def _silu(x):
    return jax.nn.silu(x)

def _sigmoid(x):
    return jax.nn.sigmoid(x)

def _layernorm(x, axis=-1, eps=1e-05):
    m = jnp.mean(x, axis=axis, keepdims=True)
    v = jnp.var(x, axis=axis, keepdims=True)
    return (x - m) / jnp.sqrt(v + eps)

def _scatter_add(tgt, idx, src, axis=0):
    return tgt.at[idx].add(src)

def _segment_sum(src, seg, n):
    return jax.ops.segment_sum(src, seg, n)
kernel_name = 'mk_cond_resid_d4_seqx_r4_663d24'

def setup_inputs(seed: int=0):
    np.random.seed(seed)
    _w = jnp.asarray

    def _rec_inputs():
        import jax
        import jax.numpy as jnp
        _rk = jax.random.key(seed)
        x = -0.000125 + 0.9999 * jax.random.normal(jax.random.fold_in(_rk, 1), (32, 64, 512), jnp.float32)
        _lenS = 64 - jax.random.randint(jax.random.fold_in(_rk, 7), (32,), 0, max(1, 64 // 4) + 1, jnp.int32)
        _lenS2 = 64 - jax.random.randint(jax.random.fold_in(_rk, 8), (32,), 0, max(1, 64 // 4) + 1, jnp.int32)
        itok_B_0_7 = jax.random.randint(jax.random.fold_in(_rk, 11), (32,), 0, 8, jnp.int32)
        fside_8xS_0 = -0.00162727 + 0.0609077 * jax.random.normal(jax.random.fold_in(_rk, 12), (8, 64), jnp.float32)
        itok_B_0_6 = jax.random.randint(jax.random.fold_in(_rk, 13), (32,), 0, 7, jnp.int32)
        itok_B_1_198 = jax.random.randint(jax.random.fold_in(_rk, 14), (32,), 1, 199, jnp.int32)
        return (x, itok_B_0_7, fside_8xS_0, itok_B_0_6, itok_B_1_198)
    x, itok_B_0_7, fside_8xS_0, itok_B_0_6, itok_B_1_198 = _rec_inputs()

    def _L0_cond_setup():
        import jax, jax.numpy as jnp
        import numpy as np
        B, C, T = (64, 64, 512)
        D, N = (64, 8)
        key = jax.random.key(seed)
        k_x, k_s, k_w, k_b = jax.random.split(key, 4)
        scale = 1.0 / np.sqrt(C)
        x = jax.random.normal(k_x, (B, C, T), dtype=jnp.float32)
        subjects = jax.random.randint(k_s, (B,), 0, N, dtype=jnp.int64)
        weights = jax.random.normal(k_w, (N, C, D), dtype=jnp.float32) * scale
        bias = jax.random.normal(k_b, (N, D), dtype=jnp.float32) * scale
        return {'x': x, 'subjects': subjects, 'weights': weights, 'bias': bias}
    _L0_cond_all = _L0_cond_setup()
    _L0_cond_in = {k: v for k, v in _L0_cond_all.items() if k in ('weights',)}
    del _L0_cond_all

    def _L1_cond_setup():
        import jax, jax.numpy as jnp
        import numpy as np

        def _lora_linear(x, W, A, B, adapter_indices):
            base = jnp.einsum('bsd,df->bsf', x, W)
            Ai = A[adapter_indices]
            Bi = B[adapter_indices]
            lora = jnp.einsum('bsr,brf->bsf', jnp.einsum('bsd,bdr->bsr', x, Ai), Bi)
            return base + lora
        key = jax.random.key(seed)
        ks = jax.random.split(key, 10)
        H, I, N, R = (512, 2048, 8, 16)
        B, S = (4, 512)
        std_h = 1.0 / np.sqrt(H)
        std_i = 1.0 / np.sqrt(I)
        x = jax.random.normal(ks[0], (B, S, H), dtype=jnp.float32)
        adapter_indices = jax.random.randint(ks[1], (B,), 0, N, dtype=jnp.int32)
        Wg = jax.random.normal(ks[2], (H, I), dtype=jnp.float32) * std_h
        Wu = jax.random.normal(ks[3], (H, I), dtype=jnp.float32) * std_h
        Wd = jax.random.normal(ks[4], (I, H), dtype=jnp.float32) * std_i
        Ag = jax.random.normal(ks[5], (N, H, R), dtype=jnp.float32) * std_h
        Bg = jnp.zeros((N, R, I), dtype=jnp.float32) + 0.01
        Au = jax.random.normal(ks[6], (N, H, R), dtype=jnp.float32) * std_h
        Bu = jnp.zeros((N, R, I), dtype=jnp.float32) + 0.01
        Ad = jax.random.normal(ks[7], (N, I, R), dtype=jnp.float32) * std_i
        Bd = jnp.zeros((N, R, H), dtype=jnp.float32) + 0.01
        return {'x': x, 'Wg': Wg, 'Wu': Wu, 'Wd': Wd, 'Ag': Ag, 'Bg': Bg, 'Au': Au, 'Bu': Bu, 'Ad': Ad, 'Bd': Bd, 'adapter_indices': adapter_indices}
    _L1_cond_all = _L1_cond_setup()
    _L1_cond_in = {k: v for k, v in _L1_cond_all.items() if k in ('Wg', 'Wu', 'Wd', 'Ag', 'Bg', 'Au', 'Bu', 'Ad', 'Bd')}
    del _L1_cond_all

    def _L2_cond_setup():
        import jax, jax.numpy as jnp
        import numpy as np
        B, T, D_IN, D_OUT = (16, 512, 512, 512)
        N_ADAPTERS, RANK = (8, 16)
        key = jax.random.key(seed)
        k_x, k_w, k_a, k_b, k_s, k_idx = jax.random.split(key, 6)
        x = jax.random.normal(k_x, (B, T, D_IN), dtype=jnp.float32)
        W = jax.random.normal(k_w, (D_OUT, D_IN), dtype=jnp.float32) * (1.0 / np.sqrt(D_IN))
        A = jax.random.normal(k_a, (N_ADAPTERS, RANK, D_IN), dtype=jnp.float32) * 0.02
        Bm = jax.random.normal(k_b, (N_ADAPTERS, D_OUT, RANK), dtype=jnp.float32) * 0.02
        scalings = jnp.ones((N_ADAPTERS,), dtype=jnp.float32)
        adapter_idx = jax.random.randint(k_idx, (B,), 0, N_ADAPTERS, dtype=jnp.int32)
        return {'x': x, 'W': W, 'A': A, 'Bm': Bm, 'scalings': scalings, 'adapter_idx': adapter_idx}
    _L2_cond_all = _L2_cond_setup()
    _L2_cond_in = {k: v for k, v in _L2_cond_all.items() if k in ('W', 'A', 'Bm', 'scalings')}
    del _L2_cond_all

    def _L3_cond_setup():
        import jax, jax.numpy as jnp
        import numpy as np
        B, C, T = (128, 64, 512)
        S, D = (200, 64)
        key = jax.random.key(seed)
        k1, k2, k3 = jax.random.split(key, 3)
        x = jax.random.normal(k1, (B, C, T), dtype=jnp.float32)
        conditions = jax.random.randint(k2, (B,), 0, S, dtype=jnp.int64)
        weights = jax.random.normal(k3, (S, C, D), dtype=jnp.float32) / jnp.sqrt(jnp.float32(C))
        return {'x': x, 'conditions': conditions, 'weights': weights}
    _L3_cond_all = _L3_cond_setup()
    _L3_cond_in = {k: v for k, v in _L3_cond_all.items() if k in ('weights',)}
    del _L3_cond_all
    return {'x': x, 'itok_B_0_7': itok_B_0_7, 'fside_8xS_0': fside_8xS_0, 'itok_B_0_6': itok_B_0_6, 'itok_B_1_198': itok_B_1_198, 'L0_cond_weights': _L0_cond_in['weights'], 'L1_cond_Wg': _L1_cond_in['Wg'], 'L1_cond_Wu': _L1_cond_in['Wu'], 'L1_cond_Wd': _L1_cond_in['Wd'], 'L1_cond_Ag': _L1_cond_in['Ag'], 'L1_cond_Bg': _L1_cond_in['Bg'], 'L1_cond_Au': _L1_cond_in['Au'], 'L1_cond_Bu': _L1_cond_in['Bu'], 'L1_cond_Ad': _L1_cond_in['Ad'], 'L1_cond_Bd': _L1_cond_in['Bd'], 'L2_cond_W': _L2_cond_in['W'], 'L2_cond_A': _L2_cond_in['A'], 'L2_cond_Bm': _L2_cond_in['Bm'], 'L2_cond_scalings': _L2_cond_in['scalings'], 'L3_cond_weights': _L3_cond_in['weights']}

def reference(x, itok_B_0_7, fside_8xS_0, itok_B_0_6, itok_B_1_198, L0_cond_weights, L1_cond_Wg, L1_cond_Wu, L1_cond_Wd, L1_cond_Ag, L1_cond_Bg, L1_cond_Au, L1_cond_Bu, L1_cond_Ad, L1_cond_Bd, L2_cond_W, L2_cond_A, L2_cond_Bm, L2_cond_scalings, L3_cond_weights):
    import jax
    import jax.numpy as jnp

    def _L0_cond_ref(x, subjects, weights, bias):
        import jax, jax.numpy as jnp
        import numpy as np
        B, C, T = (64, 64, 512)
        D, N = (64, 8)
        w = weights[subjects]
        b = bias[subjects]
        out = jnp.einsum('bct,bcd->bdt', x, w)
        out = out + b[:, :, None]
        return out

    def _L1_cond_ref(x, Wg, Wu, Wd, Ag, Bg, Au, Bu, Ad, Bd, adapter_indices):
        import jax, jax.numpy as jnp
        import numpy as np

        def _lora_linear(x, W, A, B, adapter_indices):
            base = jnp.einsum('bsd,df->bsf', x, W)
            Ai = A[adapter_indices]
            Bi = B[adapter_indices]
            lora = jnp.einsum('bsr,brf->bsf', jnp.einsum('bsd,bdr->bsr', x, Ai), Bi)
            return base + lora
        gate = _lora_linear(x, Wg, Ag, Bg, adapter_indices)
        up = _lora_linear(x, Wu, Au, Bu, adapter_indices)
        h = jax.nn.silu(gate) * up
        return _lora_linear(h, Wd, Ad, Bd, adapter_indices)

    def _L2_cond_ref(x, W, A, Bm, scalings, adapter_idx):
        import jax, jax.numpy as jnp
        import numpy as np
        B, T, D_IN, D_OUT = (16, 512, 512, 512)
        N_ADAPTERS, RANK = (8, 16)
        H = jnp.einsum('btd,od->bto', x, W)
        A_b = A[adapter_idx]
        B_b = Bm[adapter_idx]
        s_b = scalings[adapter_idx]
        xa = jnp.einsum('btd,brd->btr', x, A_b)
        delta = jnp.einsum('btr,bor->bto', xa, B_b)
        delta = jax.lax.stop_gradient(delta * s_b[:, None, None])
        return H + delta

    def _L3_cond_ref(x, conditions, weights):
        import jax, jax.numpy as jnp
        import numpy as np
        B, C, T = (128, 64, 512)
        S, D = (200, 64)
        w = weights[conditions]
        return jnp.einsum('bct,bcd->bdt', x, w)
    x = x + _L0_cond_ref(x, itok_B_0_7, L0_cond_weights, fside_8xS_0)
    x = x + _L1_cond_ref(x, L1_cond_Wg, L1_cond_Wu, L1_cond_Wd, L1_cond_Ag, L1_cond_Bg, L1_cond_Au, L1_cond_Bu, L1_cond_Ad, L1_cond_Bd, itok_B_0_7)
    x = x + _L2_cond_ref(x, L2_cond_W, L2_cond_A, L2_cond_Bm, L2_cond_scalings, itok_B_0_6)
    x = x + _L3_cond_ref(x, itok_B_1_198, L3_cond_weights)
    return x

_drawn_inputs = setup_inputs


def setup_inputs(seed=0):
    import zlib

    import numpy as np

    out = dict(_drawn_inputs(seed))
    spreads = {'L1_cond_Bg': (0.009999999776482582, 0.2),
     'L1_cond_Bu': (0.009999999776482582, 0.2),
     'L1_cond_Bd': (0.009999999776482582, 0.2),
     'L2_cond_scalings': (1.0, 0.2)}
    factors = {}
    for name, (base, spread) in spreads.items():
        noise = np.random.default_rng([zlib.crc32(name.encode()), seed]).standard_normal(out[name].shape)
        drawn = base * np.exp(spread * noise) if base else spread * noise
        out[name] = jnp.asarray(drawn.astype(out[name].dtype))
    for name, factor in factors.items():
        out[name] = (out[name] * factor).astype(out[name].dtype)
    return out
```

```python
import concourse.bass as bass
from concourse import mybir
from contextlib import ExitStack



def conditioned_residual_stack(nc, x, idx_a, bias0, idx_b, idx_c, w0, wg, wu, wd, ag, bg, au, bu, ad, bd,
                               w2, a2, b2, scal2, w3, out):
    f32, r32, i32 = mybir.dt.float32, mybir.dt.float32r, mybir.dt.int32
    u32 = mybir.dt.uint32
    ALU = mybir.AluOpType
    ACT = mybir.ActivationFunctionType
    X = mybir.AxisListType.X

    SAMPLES, POS, FEAT = x.shape
    HIDDEN = wg.shape[1]
    ADAPTERS, _, RANK = ag.shape
    P = 128
    PAIRS = SAMPLES // 2
    GP = 4
    GROUPS = PAIRS // GP
    TOK = GP * P
    KT = FEAT // P
    FT = HIDDEN // P
    SLOTS = ADAPTERS * RANK
    T = GROUPS * FT
    assert SLOTS == P and 2 * POS == P

    x_pairs = x.rearrange("b c t -> (b c) t")
    out_pairs = out.rearrange("b c t -> (b c) t")
    bg_rows = bg.rearrange("n r f -> (n r) f")
    bu_rows = bu.rearrange("n r f -> (n r) f")

    ds, ts = bass.ds, bass.ts

    ctx = ExitStack()
    with ctx:
        def sb(name, shape, dt=f32, stack=ctx):
            return stack.enter_context(nc.sbuf_tensor(name, shape, dt))

        def sem(name):
            return ctx.enter_context(nc.semaphore(name))

        bank = [ctx.enter_context(nc.psum_tensor(f"bank{i}", [P, 512], f32)) for i in range(8)]

        X1 = sb("X1", [P, PAIRS, FEAT])
        ident = sb("ident", [P, P])
        mask1 = sb("mask1", [P, SAMPLES])
        mask2 = sb("mask2", [P, SAMPLES])
        w3raw = sb("w3raw", [P, PAIRS, POS])

        main = ExitStack()
        ctx.enter_context(main)
        XT = sb("XT", [P, 2, KT, PAIRS * P], r32, main)
        UT = sb("UT", [P, 2, 2, PAIRS * P], r32, main)
        ADS = sb("ADS", [P, 2, FT, SLOTS], r32, main)
        BDS = sb("BDS", [P, 2, FEAT], r32, main)

        pa = ExitStack()
        idx = sb("idx", [P, 3, SAMPLES], i32, pa)
        idxf = sb("idxf", [P, 3, SAMPLES], f32, pa)
        row_i = sb("row_i", [P, 2, PAIRS], i32, pa)
        row_n = sb("row_n", [P, 1], f32, pa)
        lane = sb("lane", [P, PAIRS], i32, pa)
        offs = sb("offs", [P, 2, PAIRS], i32, pa)
        srow = sb("srow", [P, 1], f32, pa)
        biasT = sb("biasT", [P, ADAPTERS], f32, pa)
        napt = sb("napt", [P, ADAPTERS], i32, pa)
        naptf = sb("naptf", [P, ADAPTERS], f32, pa)
        beq = sb("beq", [P, PAIRS, ADAPTERS], f32, pa)
        bias = sb("bias", [P, PAIRS], f32, pa)
        agu_raw = sb("agu_raw", [P, 2, KT, SLOTS], f32, pa)
        AGU = sb("AGU", [P, 2, 2, KT, SLOTS], r32, pa)
        ad_raw = sb("ad_raw", [P, FT, SLOTS], f32, pa)
        bd_raw = sb("bd_raw", [P, FEAT], f32, pa)
        w0raw = sb("w0raw", [P, PAIRS, POS], f32, pa)
        w0bd = [sb(f"w0bd{s}", [P, 2, P], r32, pa) for s in range(2)]
        xs = [sb(f"xs{s}", [P, FEAT], f32, pa) for s in range(2)]
        xh = [sb(f"xh{s}", [P, 2, FEAT], r32, pa) for s in range(2)]
        x1s = [sb(f"x1s{s}", [P, FEAT], f32, pa) for s in range(2)]
        ut = [sb(f"ut{s}", [P, 2, P], f32, pa) for s in range(2)]

        s_idx, s_tab, s_dch, s_pch = sem("s_idx"), sem("s_tab"), sem("s_dch"), sem("s_pch")
        s_consts, s_ident, s_offs, s_idxc = sem("s_consts"), sem("s_ident"), sem("s_offs"), sem("s_idxc")
        s_zero, s_prep, s_tabh, s_tabl = sem("s_zero"), sem("s_prep"), sem("s_tabh"), sem("s_tabl")
        s_xload = [sem(f"s_xload{s}") for s in range(2)]
        s_xkept = [sem(f"s_xkept{s}") for s in range(2)]
        s_w0 = [sem(f"s_w0_{s}") for s in range(2)]
        s_w3 = sem("s_w3")
        s_xh, s_w0h, s_xsplit, s_l0, s_x1 = sem("s_xh"), sem("s_w0h"), sem("s_xsplit"), sem("s_l0"), sem("s_x1")
        s_tr, s_xth, s_xtl, s_u, s_um, s_uh, s_ul = (sem(n) for n in
            ("s_tr", "s_xth", "s_xtl", "s_u", "s_um", "s_uh", "s_ul"))

        psL0, psT, psU = bank[0:2], bank[2:4], bank[4:6]

        with nc.Block() as block:

            @block.sync
            def _(sp):
                for n, v in enumerate((idx_a, idx_b, idx_c)):
                    sp.dma_start(idx[:, n, :], v.partition_broadcast(P)).then_inc(s_idx, 16)
                for s in range(2):
                    sp.dma_start(xs[s][:, :], x_pairs[s * P:(s + 1) * P, :]).then_inc(s_xload[s], 16)

                def keep(p, s):
                    sp.wait_ge(s_x1, p + 1)
                    sp.dma_start(X1[:, ds(p, 1), :], x1s[s][:, :]).then_inc(s_xkept[s], 16)

                with sp.Fori(0, PAIRS // 2 - 1) as i:
                    for s in range(2):
                        keep(2 * i + s, s)
                        sp.dma_start(xs[s][:, :], x_pairs[ds((2 * i + s + 2) * P, P), :]).then_inc(s_xload[s], 16)
                for s in range(2):
                    keep(PAIRS - 2 + s, s)
                for s in range(2):
                    sp.wait_ge(s_xkept[s], 16 * PAIRS // 2)

            @block.gpsimd
            def _(pool):
                nc.gpsimd.memset(ident[:, :], 0.0).then_inc(s_pch, 1)
                nc.gpsimd.iota(row_i[:, 0, 0:1], [[0, 1]], base=0, channel_multiplier=1).then_inc(s_consts, 1)
                nc.gpsimd.iota(lane[:, :], [[0, PAIRS]], base=0, channel_multiplier=1).then_inc(s_consts, 1)
                nc.gpsimd.iota(napt[:, :], [[1, ADAPTERS]], base=0, channel_multiplier=0).then_inc(s_consts, 1)
                pool.wait_ge(s_pch, 1)
                nc.gpsimd.affine_select(out=ident[:, :], in_=ident[:, :], compare_op=ALU.not_equal, fill=1.0, base=0,
                                        pattern=[[-1, P]], channel_multiplier=1).then_inc(s_ident, 1)
                pool.wait_ge(s_offs, 2)
                rows0 = w0.rearrange("n c d -> (n c) d")
                rows3 = w3.rearrange("n c d -> (n c) d")
                for p in range(PAIRS):
                    s = p % 2
                    if p >= 2:
                        pool.wait_ge(s_w0[s], 16 * (p // 2))
                    nc.gpsimd.indirect_dma_start(
                        w0raw[:, p, :], None, rows0,
                        bass.IndirectOffsetOnAxis(offs[:, 0, p:p + 1].bitcast(u32), 0)).then_inc(s_w0[s], 16)
                for p in range(PAIRS):
                    nc.gpsimd.indirect_dma_start(
                        w3raw[:, p, :], None, rows3,
                        bass.IndirectOffsetOnAxis(offs[:, 1, p:p + 1].bitcast(u32), 0)).then_inc(s_w3, 16)
                pool.wait_ge(s_w3, 16 * PAIRS)

            @block.scalar
            def _(act):
                with nc.allow_non_contiguous_dma(reason="512 values, once"):
                    for s in range(2):
                        act.dma_start(biasT[s * POS:(s + 1) * POS, :], bias0.rearrange("n d -> d n")).then_inc(s_idx, 16)
                for n in range(ADAPTERS):
                    act.dma_start(srow[n * RANK:(n + 1) * RANK, :], scal2[n:n + 1].partition_broadcast(RANK)).then_inc(s_idx, 16)
                for j, a in enumerate((ag, au)):
                    for n in range(ADAPTERS):
                        act.dma_start(agu_raw[:, j, :, n * RANK:(n + 1) * RANK],
                                      a[n].rearrange("(k p) r -> p k r", p=P)).then_inc(s_tab, 16)
                for n in range(ADAPTERS):
                    act.dma_start(ad_raw[:, :, n * RANK:(n + 1) * RANK],
                                  ad[n].rearrange("(k p) r -> p k r", p=P)).then_inc(s_tab, 16)
                act.dma_start(bd_raw[:, :], bd.rearrange("n r f -> (n r) f")).then_inc(s_tab, 16)

                def x_high(p, s, n):
                    act.wait_ge(s_xload[s], 16 * (n + 1))
                    if not isinstance(p, int) or p >= 2:
                        act.wait_ge(s_l0, p - 1)
                    nc.scalar.activation(xh[s][:, 0, :], xs[s][:, :], ACT.Copy).then_inc(s_xh, 1)
                    act.wait_ge(s_w0[s], 16 * (n + 1))
                    for h in range(2):
                        last = nc.scalar.activation(w0bd[s][h * POS:(h + 1) * POS, 0, h * POS:(h + 1) * POS],
                                                    w0raw[h * POS:(h + 1) * POS, ds(p, 1), :], ACT.Copy)
                    last.then_inc(s_w0h, 1)

                def xt_high(p, s):
                    act.wait_ge(s_tr, p + 1)
                    nc.scalar.activation(XT[:, 0, :, ds(p * P, P)],
                                         psT[s][:, :].rearrange("p (k t) -> p k t", k=KT), ACT.Copy).then_inc(s_xth, 1)

                def u_high(p, s):
                    act.wait_ge(s_um, p + 1)
                    nc.scalar.activation(UT[:, :, 0, ds(p * P, P)], ut[s][:, :, :], ACT.Copy).then_inc(s_uh, 1)

                act.wait_ge(s_zero, 2)
                x_high(0, 0, 0)
                act.wait_ge(s_tab, 16 * (3 * ADAPTERS + 1))
                nc.scalar.activation(AGU[:, 0, :, :, :], agu_raw[:, :, :, :], ACT.Copy).then_inc(s_tabh, 1)
                x_high(1, 1, 0)
                xt_high(0, 0)
                nc.scalar.activation(ADS[:, 0, :, :], ad_raw[:, :, :], ACT.Copy).then_inc(s_tabh, 1)
                nc.scalar.activation(BDS[:, 0, :], bd_raw[:, :], ACT.Copy).then_inc(s_tabh, 1)
                def pairs(i):
                    for s in range(2):
                        p = 2 * i + s
                        x_high(p, s, i)
                        xt_high(p - 1, 1 - s)
                        u_high(p - 2, s)

                pairs(1)
                with act.Fori(2, PAIRS // 2) as i:
                    pairs(i)
                xt_high(PAIRS - 1, 1)
                u_high(PAIRS - 2, 0)
                u_high(PAIRS - 1, 1)

            @block.vector
            def _(dve):
                chain = [0]

                def link(ins):
                    chain[0] += 1
                    ins.then_inc(s_dch, 1)
                    dve.wait_ge(s_dch, chain[0])

                for s in range(2):
                    nc.vector.memset(w0bd[s][:, :, :].bitcast(f32), 0.0).then_inc(s_zero, 1)
                dve.wait_ge(s_consts, 3)
                dve.wait_ge(s_idx, 16 * (3 + 2 + ADAPTERS))
                link(nc.vector.tensor_scalar(lane[:, :], lane[:, :], POS - 1, None, ALU.bitwise_and))
                for h in range(2):
                    rows = slice(h * POS, (h + 1) * POS)
                    for j, n in ((0, 0), (1, 2)):
                        link(nc.vector.tensor_scalar(offs[rows, j, :],
                                                     idx[rows, n, :].rearrange("p (q h) -> p q h", h=2)[:, :, h],
                                                     POS.bit_length() - 1, None, ALU.logical_shift_left))
                for j in range(2):
                    nc.vector.tensor_tensor(offs[:, j, :], offs[:, j, :], lane[:, :], ALU.add).then_inc(s_offs, 1)
                link(nc.vector.tensor_scalar(row_i[:, 1, 0:1], row_i[:, 0, 0:1], RANK.bit_length() - 1, None,
                                             ALU.logical_shift_right))
                link(nc.vector.tensor_copy(row_n[:, :], row_i[:, 1, 0:1]))
                link(nc.vector.tensor_copy(idxf[:, :, :], idx[:, :, :]))
                link(nc.vector.tensor_copy(naptf[:, :], napt[:, :]))
                nc.vector.tensor_scalar(mask1[:, :], idxf[:, 0, :], row_n[:, 0:1], None, ALU.is_equal)
                nc.vector.tensor_scalar(mask2[:, :], idxf[:, 1, :], row_n[:, 0:1], srow[:, 0:1],
                                        ALU.is_equal, ALU.mult)
                for h in range(2):
                    rows = slice(h * POS, (h + 1) * POS)
                    sel = idxf[rows, 0, :].rearrange("p (q h) -> p q h", h=2)[:, :, h:h + 1]
                    link(nc.vector.tensor_tensor(beq[rows, :, :], sel.to_broadcast([POS, PAIRS, ADAPTERS]),
                                                 naptf[rows, :].unsqueeze(1).to_broadcast([POS, PAIRS, ADAPTERS]),
                                                 ALU.is_equal))
                link(nc.vector.tensor_tensor(beq[:, :, :], beq[:, :, :],
                                             biasT[:, :].unsqueeze(1).to_broadcast([P, PAIRS, ADAPTERS]), ALU.mult))
                link(nc.vector.tensor_reduce(bias[:, :], beq[:, :, :], X, ALU.add))

                def x_low(p, s):
                    dve.wait_ge(s_xh, p + 1)
                    nc.vector.tensor_tensor(xh[s][:, 1, :], xs[s][:, :], xh[s][:, 0, :].bitcast(f32), ALU.subtract)
                    dve.wait_ge(s_w0h, p + 1)
                    for h in range(2):
                        rows = slice(h * POS, (h + 1) * POS)
                        last = nc.vector.tensor_tensor(w0bd[s][rows, 1, rows], w0raw[rows, ds(p, 1), :].rearrange("p a d -> p (a d)"),
                                                       w0bd[s][rows, 0, rows].bitcast(f32), ALU.subtract)
                    last.then_inc(s_xsplit, 1)

                def x1(p, s, n):
                    dve.wait_ge(s_l0, p + 1)
                    if not isinstance(p, int) or p >= 2:
                        dve.wait_ge(s_tr, p - 1)
                        dve.wait_ge(s_xkept[s], 16 * n)
                    nc.vector.scalar_tensor_tensor(out=x1s[s][:, :], in0=psL0[s][:, :], scalar=bias[:, ds(p, 1)],
                                                   in1=xs[s][:, :], op0=ALU.add, op1=ALU.add).then_inc(s_x1, 1)

                def xt_low(p, s):
                    dve.wait_ge(s_xth, p + 1)
                    nc.vector.tensor_tensor(XT[:, 1, :, ds(p * P, P)],
                                            psT[s][:, :].rearrange("p (k t) -> p k t", k=KT),
                                            XT[:, 0, :, ds(p * P, P)].bitcast(f32), ALU.subtract).then_inc(s_xtl, 1)

                def u_mask(p, s):
                    dve.wait_ge(s_u, p + 1)
                    for j in range(2):
                        last = nc.vector.tensor_tensor(
                            ut[s][:, j, :].rearrange("p (b t) -> p b t", b=2),
                            psU[s][:, j * P:(j + 1) * P].rearrange("p (b t) -> p b t", b=2),
                            mask1[:, ds(2 * p, 2)].unsqueeze(2).to_broadcast([P, 2, POS]), ALU.mult)
                    last.then_inc(s_um, 1)

                def u_low(p, s):
                    dve.wait_ge(s_uh, p + 1)
                    nc.vector.tensor_tensor(UT[:, :, 1, ds(p * P, P)], ut[s][:, :, :],
                                            UT[:, :, 0, ds(p * P, P)].bitcast(f32), ALU.subtract).then_inc(s_ul, 1)

                x_low(0, 0)
                x1(0, 0, 0)
                dve.wait_ge(s_tabh, 1)
                nc.vector.tensor_tensor(AGU[:, 1, :, :, :], agu_raw[:, :, :, :], AGU[:, 0, :, :, :].bitcast(f32),
                                        ALU.subtract).then_inc(s_tabl, 1)
                x_low(1, 1)
                x1(1, 1, 0)
                xt_low(0, 0)
                dve.wait_ge(s_tabh, 3)
                nc.vector.tensor_tensor(ADS[:, 1, :, :], ad_raw[:, :, :], ADS[:, 0, :, :].bitcast(f32), ALU.subtract)
                nc.vector.tensor_tensor(BDS[:, 1, :], bd_raw[:, :], BDS[:, 0, :].bitcast(f32),
                                        ALU.subtract).then_inc(s_tabl, 1)
                def pairs(i):
                    for s in range(2):
                        p = 2 * i + s
                        x_low(p, s)
                        u_mask(p - 2, s)
                        x1(p, s, i)
                        xt_low(p - 1, 1 - s)
                        u_low(p - 2, s)

                pairs(1)
                with dve.Fori(2, PAIRS // 2) as i:
                    pairs(i)
                xt_low(PAIRS - 1, 1)
                for p in (PAIRS - 2, PAIRS - 1):
                    u_mask(p, p % 2)
                    u_low(p, p % 2)

            @block.tensor
            def _(pe):
                def layer0(p, s):
                    pe.wait_ge(s_xsplit, p + 1)
                    if not isinstance(p, int) or p >= 2:
                        pe.wait_ge(s_x1, p - 1)
                    for n, (a, b) in enumerate(((0, 0), (0, 1), (1, 0))):
                        last = nc.tensor.matmul(psL0[s][:, :], w0bd[s][:, a, :], xh[s][:, b, :], start=(n == 0), stop=(n == 2))
                    last.then_inc(s_l0, 1)

                def transposes(p, s):
                    pe.wait_ge(s_x1, p + 1)
                    if not isinstance(p, int) or p >= 2:
                        pe.wait_ge(s_xtl, p - 1)
                    for k in range(KT):
                        last = nc.tensor.transpose(psT[s][:, k * P:(k + 1) * P], x1s[s][:, k * P:(k + 1) * P], ident[:, :])
                    last.then_inc(s_tr, 1)

                def lora_in(p, s):
                    pe.wait_ge(s_xtl, p + 1)
                    if not isinstance(p, int) or p >= 2:
                        pe.wait_ge(s_um, p - 1)
                    for j in range(2):
                        for k in range(KT):
                            for n, (a, b) in enumerate(((0, 0), (0, 1), (1, 0))):
                                last = nc.tensor.matmul(psU[s][:, j * P:(j + 1) * P], AGU[:, a, j, k, :],
                                                        XT[:, b, k, ds(p * P, P)],
                                                        start=(k == 0 and n == 0), stop=(k == KT - 1 and n == 2))
                    last.then_inc(s_u, 1)

                layer0(0, 0)
                layer0(1, 1)
                pe.wait_ge(s_ident, 1)
                transposes(0, 0)
                pe.wait_ge(s_tabl, 1)
                def pairs(i):
                    for s in range(2):
                        p = 2 * i + s
                        layer0(p, s)
                        transposes(p - 1, 1 - s)
                        lora_in(p - 2, s)

                pairs(1)
                with pe.Fori(2, PAIRS // 2) as i:
                    pairs(i)
                transposes(PAIRS - 1, 1)
                lora_in(PAIRS - 2, 0)
                lora_in(PAIRS - 1, 1)

        pa.close()

        GU = 2 * (KT + 1) * P
        stage = [sb(f"stage{s}", [P, GU + FEAT], f32, main) for s in range(2)]
        gu = [sb(f"gu{s}", [P, 2, 2, KT + 1, P], r32, main) for s in range(2)]
        wds = [sb(f"wds{s}", [P, 2, FEAT], r32, main) for s in range(2)]
        hid = [sb(f"hid{s}", [P, TOK], f32, main) for s in range(2)]
        hs = [sb(f"hs{s}", [P, 2, TOK], r32, main) for s in range(2)]
        udc = sb("udc", [P, TOK], f32, main)
        uds = sb("uds", [P, 2, TOK], r32, main)

        psG, psUp, psD, psUd, psUdT = bank[0], bank[1], bank[2:6], bank[6], bank[7]

        s_wload = [sem(f"s_wload{s}") for s in range(2)]
        s_guh, s_gul, s_wdh, s_wdl = sem("s_guh"), sem("s_gul"), sem("s_wdh"), sem("s_wdl")
        s_gate, s_silu, s_up, s_hid, s_hh, s_hl, s_down = (sem(n) for n in
            ("s_gate", "s_silu", "s_up", "s_hid", "s_hh", "s_hl", "s_down"))
        s_udc, s_udt, s_udm, s_udh, s_udl, s_lb, s_x2 = (sem(n) for n in
            ("s_udc", "s_udt", "s_udm", "s_udh", "s_udl", "s_lb", "s_x2"))
        DMAS = 5

        with nc.Block() as block:

            @block.sync
            def _(sp):
                def load(f, s):
                    g2 = stage[s][:, 0:GU].rearrange("p (j k f) -> p j k f", j=2, k=KT + 1)
                    cols = ds(f * P, P)
                    for j, (w, b) in enumerate(((wg, bg_rows), (wu, bu_rows))):
                        sp.dma_start(g2[:, j, 0:KT, :], w.rearrange("(k p) f -> p k f", p=P)[:, :, cols]).then_inc(s_wload[s], 16)
                        sp.dma_start(g2[:, j, KT, :], b[:, cols]).then_inc(s_wload[s], 16)
                    sp.dma_start(stage[s][:, GU:GU + FEAT], wd[cols, :]).then_inc(s_wload[s], 16)

                load(0, 0)
                load(1, 1)
                with sp.Fori(1, FT // 2) as i:
                    for s in range(2):
                        sp.wait_ge(s_wdl, 2 * i + s - 1)
                        sp.wait_ge(s_gul, 2 * i + s - 1)
                        load(2 * i + s, s)
                with sp.Fori(1, GROUPS) as g:
                    with sp.Fori(0, FT // 2) as i:
                        for s in range(2):
                            sp.wait_ge(s_wdl, FT * g + 2 * i + s - 1)
                            sp.wait_ge(s_gul, FT * g + 2 * i + s - 1)
                            load(2 * i + s, s)

            @block.scalar
            def _(act):
                def gu_high(t, s, n):
                    act.wait_ge(s_wload[s], 16 * DMAS * (n + 1))
                    if not isinstance(t, int) or t >= 2:
                        act.wait_ge(s_up, t - 1)
                    nc.scalar.activation(gu[s][:, 0, :, :, :].rearrange("p j k f -> p (j k f)"),
                                         stage[s][:, 0:GU], ACT.Copy).then_inc(s_guh, 1)

                def wd_high(t, s):
                    if not isinstance(t, int) or t >= 2:
                        act.wait_ge(s_down, t - 1)
                    nc.scalar.activation(wds[s][:, 0, :], stage[s][:, GU:GU + FEAT], ACT.Copy).then_inc(s_wdh, 1)

                def silu(t, s):
                    act.wait_ge(s_gate, t + 1)
                    if not isinstance(t, int) or t >= 2:
                        act.wait_ge(s_hl, t - 1)
                    nc.scalar.activation(hid[s][:, :], psG[:, :], ACT.Silu).then_inc(s_silu, 1)

                def hid_high(t, s):
                    act.wait_ge(s_hid, t + 1)
                    if not isinstance(t, int) or t >= 2:
                        act.wait_ge(s_down, t - 1)
                    nc.scalar.activation(hs[s][:, 0, :], hid[s][:, :], ACT.Copy).then_inc(s_hh, 1)

                def step(t, s, n):
                    gu_high(t, s, n)
                    wd_high(t - 1, 1 - s)
                    silu(t - 1, 1 - s)

                def ud_copy(g):
                    act.wait_ge(s_down, FT * g + FT)
                    if not isinstance(g, int) or g >= 1:
                        act.wait_ge(s_udl, g)
                    nc.scalar.activation(udc[:, :], psUd[:, :], ACT.Copy).then_inc(s_udc, 1)

                def ud_high(g):
                    act.wait_ge(s_udm, g + 1)
                    if not isinstance(g, int) or g >= 1:
                        act.wait_ge(s_lb, g)
                    nc.scalar.activation(uds[:, 0, :], udc[:, :], ACT.Copy).then_inc(s_udh, 1)

                def inner(t0, n0):
                    with act.Fori(1, FT // 2) as i:
                        for s in range(2):
                            step(t0 + 2 * i + s, s, n0 + i)
                            hid_high(t0 + 2 * i + s - 1, 1 - s)

                gu_high(0, 0, 0)
                step(1, 1, 0)
                hid_high(0, 0)
                inner(0, 0)
                with act.Fori(1, GROUPS) as g:
                    t0, n0 = FT * g, FT // 2 * g
                    step(t0, 0, n0)
                    hid_high(t0 - 1, 1)
                    step(t0 + 1, 1, n0)
                    ud_copy(g - 1)
                    hid_high(t0, 0)
                    ud_high(g - 1)
                    inner(t0, n0)
                wd_high(T - 1, 1)
                silu(T - 1, 1)
                hid_high(T - 1, 1)
                ud_copy(GROUPS - 1)
                ud_high(GROUPS - 1)

            @block.vector
            def _(dve):
                def gu_low(t, s):
                    dve.wait_ge(s_guh, t + 1)
                    nc.vector.tensor_tensor(gu[s][:, 1, :, :, :].rearrange("p j k f -> p (j k f)"), stage[s][:, 0:GU],
                                            gu[s][:, 0, :, :, :].rearrange("p j k f -> p (j k f)").bitcast(f32),
                                            ALU.subtract).then_inc(s_gul, 1)

                def wd_low(t, s):
                    dve.wait_ge(s_wdh, t + 1)
                    nc.vector.tensor_tensor(wds[s][:, 1, :], stage[s][:, GU:GU + FEAT], wds[s][:, 0, :].bitcast(f32),
                                            ALU.subtract).then_inc(s_wdl, 1)

                def gated(t, s):
                    dve.wait_ge(s_up, t + 1)
                    dve.wait_ge(s_silu, t + 1)
                    nc.vector.tensor_tensor(hid[s][:, :], psUp[:, :], hid[s][:, :], ALU.mult).then_inc(s_hid, 1)

                def hid_low(t, s):
                    dve.wait_ge(s_hh, t + 1)
                    nc.vector.tensor_tensor(hs[s][:, 1, :], hid[s][:, :], hs[s][:, 0, :].bitcast(f32),
                                            ALU.subtract).then_inc(s_hl, 1)

                def ud_mask(g):
                    dve.wait_ge(s_udt, g + 1)
                    nc.vector.tensor_tensor(udc[:, :].rearrange("p (b t) -> p b t", t=POS),
                                            psUdT[:, :].rearrange("p (b t) -> p b t", t=POS),
                                            mask1[:, ds(2 * GP * g, 2 * GP)].unsqueeze(2).to_broadcast([P, 2 * GP, POS]),
                                            ALU.mult).then_inc(s_udm, 1)
                    dve.wait_ge(s_udh, g + 1)
                    nc.vector.tensor_tensor(uds[:, 1, :], udc[:, :], uds[:, 0, :].bitcast(f32),
                                            ALU.subtract).then_inc(s_udl, 1)

                def x2(g):
                    dve.wait_ge(s_lb, g + 1)
                    for j in range(GP):
                        dst = X1[:, ds(GP * g + j, 1), :].rearrange("p a f -> p (a f)")
                        last = nc.vector.tensor_tensor(dst, psD[j][:, :], dst, ALU.add)
                    last.then_inc(s_x2, 1)

                def step(t, s):
                    gu_low(t, s)
                    wd_low(t - 1, 1 - s)
                    gated(t - 1, 1 - s)
                    hid_low(t - 1, 1 - s)

                def inner(t0):
                    with dve.Fori(1, FT // 2) as i:
                        for s in range(2):
                            step(t0 + 2 * i + s, s)

                gu_low(0, 0)
                step(1, 1)
                inner(0)
                with dve.Fori(1, GROUPS) as g:
                    step(FT * g, 0)
                    step(FT * g + 1, 1)
                    ud_mask(g - 1)
                    x2(g - 1)
                    inner(FT * g)
                wd_low(T - 1, 1)
                gated(T - 1, 1)
                hid_low(T - 1, 1)
                ud_mask(GROUPS - 1)
                x2(GROUPS - 1)

            @block.tensor
            def _(pe):
                def half(j, t, s, g, psum, done):
                    for k in range(KT + 1):
                        for n, (a, b) in enumerate(((0, 0), (0, 1), (1, 0))):
                            src = XT[:, b, k, ds(g * TOK, TOK)] if k < KT else UT[:, j, b, ds(g * TOK, TOK)]
                            last = nc.tensor.matmul(psum[:, :], gu[s][:, a, j, k, :], src,
                                                    start=(k == 0 and n == 0), stop=(k == KT and n == 2))
                    last.then_inc(done, 1)

                def gate(t, s, g):
                    pe.wait_ge(s_gul, t + 1)
                    if not isinstance(t, int) or t >= 1:
                        pe.wait_ge(s_silu, t)
                    half(0, t, s, g, psG, s_gate)

                def up(t, s, g):
                    if not isinstance(t, int) or t >= 1:
                        pe.wait_ge(s_hid, t)
                    half(1, t, s, g, psUp, s_up)

                def down(t, s, f, first=False):
                    pe.wait_ge(s_hl, t + 1)
                    pe.wait_ge(s_wdl, t + 1)
                    for j in range(GP):
                        for a in range(2):
                            lhs = hs[s][:, a, j * P:(j + 1) * P]
                            for b in range(2 - a):
                                nc.tensor.matmul(psD[j][:, :], lhs, wds[s][:, b, :],
                                                 start=(first and a == 0 and b == 0), stop=False)
                                last = nc.tensor.matmul(psUd[:, j * P:(j + 1) * P], lhs, ADS[:, b, ds(f, 1), :].rearrange("p a f -> p (a f)"),
                                                        start=(first and j == 0 and a == 0 and b == 0), stop=False,
                                                        skip_group_check=True)
                    last.then_inc(s_down, 1)

                def ud_transposes(g):
                    pe.wait_ge(s_udc, g + 1)
                    for j in range(GP):
                        last = nc.tensor.transpose(psUdT[:, j * P:(j + 1) * P], udc[:, j * P:(j + 1) * P], ident[:, :])
                    last.then_inc(s_udt, 1)

                def lora_down(g):
                    pe.wait_ge(s_udl, g + 1)
                    for j in range(GP):
                        for n, (a, b) in enumerate(((0, 0), (0, 1), (1, 0))):
                            last = nc.tensor.matmul(psD[j][:, :], uds[:, a, j * P:(j + 1) * P], BDS[:, b, :],
                                                    start=False, stop=(n == 2))
                    last.then_inc(s_lb, 1)

                def inner(t0, g):
                    with pe.Fori(1, FT // 2) as i:
                        for s in range(2):
                            t = t0 + 2 * i + s
                            gate(t, s, g)
                            up(t, s, g)
                            down(t - 1, 1 - s, 2 * i + s - 1)

                gate(0, 0, 0)
                up(0, 0, 0)
                gate(1, 1, 0)
                up(1, 1, 0)
                down(0, 0, 0, first=True)
                inner(0, 0)
                with pe.Fori(1, GROUPS) as g:
                    t0 = FT * g
                    gate(t0, 0, g)
                    down(t0 - 1, 1, FT - 1)
                    up(t0, 0, g)
                    gate(t0 + 1, 1, g)
                    ud_transposes(g - 1)
                    up(t0 + 1, 1, g)
                    lora_down(g - 1)
                    pe.wait_ge(s_x2, g)
                    down(t0, 0, 0, first=True)
                    inner(t0, g)
                down(T - 1, 1, FT - 1)
                ud_transposes(GROUPS - 1)
                lora_down(GROUPS - 1)

        main.close()

        pc = ctx
        w2_raw = sb("w2_raw", [P, KT, FEAT])
        a2_raw = sb("a2_raw", [P, FEAT])
        b2_raw = sb("b2_raw", [P, KT, SLOTS])
        W2T = sb("W2T", [P, 2, KT, FEAT], r32)
        A2T = sb("A2T", [P, 2, KT, SLOTS], r32)
        B2T = sb("B2T", [P, 2, FEAT], r32)
        x2s = [sb(f"x2s{s}", [P, FEAT]) for s in range(2)]
        x2t = [sb(f"x2t{s}", [P, 2, KT, P], r32) for s in range(2)]
        u2 = [sb(f"u2_{s}", [P, P]) for s in range(2)]
        u2s = [sb(f"u2s{s}", [P, 2, P], r32) for s in range(2)]
        x3 = [sb(f"x3_{s}", [P, FEAT]) for s in range(2)]
        x3s = [sb(f"x3s{s}", [P, 2, FEAT], r32) for s in range(2)]
        w3bd = [sb(f"w3bd{s}", [P, 2, P], r32) for s in range(2)]
        y = [sb(f"y{s}", [P, FEAT]) for s in range(2)]

        pT, pU, pL2, pL3 = bank[0:2], bank[2:4], bank[4:6], bank[6:8]
        c_tab = sem("c_tab")
        c_tt, c_th, c_tl, c_zero = sem("c_tt"), sem("c_th"), sem("c_tl"), sem("c_zero")
        c_x2 = [sem(f"c_x2_{s}") for s in range(2)]
        c_out = [sem(f"c_out{s}") for s in range(2)]
        c_tr, c_xh, c_xl, c_u, c_um, c_uh, c_ul, c_l2, c_x3, c_x3h, c_x3l, c_w3h, c_w3l, c_l3, c_y = (sem(n) for n in
            ("c_tr", "c_xh", "c_xl", "c_u", "c_um", "c_uh", "c_ul", "c_l2", "c_x3", "c_x3h", "c_x3l", "c_w3h", "c_w3l",
             "c_l3", "c_y"))
        TABS = KT + 2

        with nc.Block() as block:

            @block.sync
            def _(sp):
                def load(p, s):
                    sp.dma_start(x2s[s][:, :], X1[:, ds(p, 1), :]).then_inc(c_x2[s], 16)

                load(0, 0)
                load(1, 1)

                def store(p, s):
                    sp.wait_ge(c_y, p + 1)
                    sp.dma_start(out_pairs[ds(p * P, P), :], y[s][:, :]).then_inc(c_out[s], 16)

                with sp.Fori(0, PAIRS // 2 - 1) as i:
                    for s in range(2):
                        p = 2 * i + s
                        sp.wait_ge(c_x3, p + 1)
                        load(p + 2, s)
                        store(p, s)
                for s in range(2):
                    store(PAIRS - 2 + s, s)
                for s in range(2):
                    sp.wait_ge(c_out[s], 16 * PAIRS // 2)

            @block.scalar
            def _(act):
                act.dma_start(w2_raw[:, :, :], w2.rearrange("(k p) f -> p k f", p=P)).then_inc(c_tab, 16)
                act.dma_start(a2_raw[:, :], a2.rearrange("n r f -> (n r) f")).then_inc(c_tab, 16)
                for n in range(ADAPTERS):
                    act.dma_start(b2_raw[:, :, n * RANK:(n + 1) * RANK],
                                  b2[n].rearrange("(k p) r -> p k r", p=P)).then_inc(c_tab, 16)
                for n in range(TABS):
                    act.wait_ge(c_tt, n + 1)
                    dst = W2T[:, 0, n, :] if n < KT else A2T[:, 0, :, :].rearrange("p k f -> p (k f)") if n == KT else B2T[:, 0, :]
                    nc.scalar.activation(dst, bank[n][:, :], ACT.Copy).then_inc(c_th, 1)

                def xt_high(p, s):
                    act.wait_ge(c_tr, p + 1)
                    if not isinstance(p, int) or p >= 2:
                        act.wait_ge(c_l2, p - 1)
                    nc.scalar.activation(x2t[s][:, 0, :, :].rearrange("p k t -> p (k t)"), pT[s][:, :], ACT.Copy).then_inc(c_xh, 1)

                def w3_high(p, s):
                    if not isinstance(p, int) or p >= 2:
                        act.wait_ge(c_l3, p - 1)
                    for h in range(2):
                        rows = slice(h * POS, (h + 1) * POS)
                        last = nc.scalar.activation(w3bd[s][rows, 0, rows], w3raw[rows, ds(p, 1), :], ACT.Copy)
                    last.then_inc(c_w3h, 1)

                def u_high(p, s):
                    act.wait_ge(c_um, p + 1)
                    nc.scalar.activation(u2s[s][:, 0, :], u2[s][:, :], ACT.Copy).then_inc(c_uh, 1)

                def x3_high(p, s):
                    act.wait_ge(c_x3, p + 1)
                    if not isinstance(p, int) or p >= 2:
                        act.wait_ge(c_l3, p - 1)
                    nc.scalar.activation(x3s[s][:, 0, :], x3[s][:, :], ACT.Copy).then_inc(c_x3h, 1)

                act.wait_ge(c_zero, 2)
                xt_high(0, 0)
                w3_high(0, 0)
                xt_high(1, 1)
                w3_high(1, 1)
                u_high(0, 0)
                def pairs(i):
                    for s in range(2):
                        p = 2 * i + s
                        xt_high(p, s)
                        x3_high(p - 2, s)
                        w3_high(p, s)
                        u_high(p - 1, 1 - s)

                pairs(1)
                with act.Fori(2, PAIRS // 2) as i:
                    pairs(i)
                x3_high(PAIRS - 2, 0)
                u_high(PAIRS - 1, 1)
                x3_high(PAIRS - 1, 1)

            @block.vector
            def _(dve):
                for s in range(2):
                    nc.vector.memset(w3bd[s][:, :, :].bitcast(f32), 0.0).then_inc(c_zero, 1)
                for n in range(TABS):
                    dve.wait_ge(c_th, n + 1)
                    t = (W2T[:, :, n, :] if n < KT else A2T[:, :, :, :].rearrange("p a k f -> p a (k f)") if n == KT else B2T[:, :, :])
                    nc.vector.tensor_tensor(t[:, 1, :], bank[n][:, :], t[:, 0, :].bitcast(f32), ALU.subtract).then_inc(c_tl, 1)

                def xt_low(p, s):
                    dve.wait_ge(c_xh, p + 1)
                    nc.vector.tensor_tensor(x2t[s][:, 1, :, :].rearrange("p k t -> p (k t)"), pT[s][:, :],
                                            x2t[s][:, 0, :, :].rearrange("p k t -> p (k t)").bitcast(f32),
                                            ALU.subtract).then_inc(c_xl, 1)

                def w3_low(p, s):
                    dve.wait_ge(c_w3h, p + 1)
                    for h in range(2):
                        rows = slice(h * POS, (h + 1) * POS)
                        last = nc.vector.tensor_tensor(w3bd[s][rows, 1, rows], w3raw[rows, ds(p, 1), :].rearrange("p a d -> p (a d)"),
                                                       w3bd[s][rows, 0, rows].bitcast(f32), ALU.subtract)
                    last.then_inc(c_w3l, 1)

                def u_mask(p, s):
                    dve.wait_ge(c_u, p + 1)
                    nc.vector.tensor_tensor(u2[s][:, :].rearrange("p (b t) -> p b t", b=2),
                                            pU[s][:, 0:P].rearrange("p (b t) -> p b t", b=2),
                                            mask2[:, ds(2 * p, 2)].unsqueeze(2).to_broadcast([P, 2, POS]),
                                            ALU.mult).then_inc(c_um, 1)
                    dve.wait_ge(c_uh, p + 1)
                    nc.vector.tensor_tensor(u2s[s][:, 1, :], u2[s][:, :], u2s[s][:, 0, :].bitcast(f32),
                                            ALU.subtract).then_inc(c_ul, 1)

                def x3_sum(p, s):
                    dve.wait_ge(c_l2, p + 1)
                    nc.vector.tensor_tensor(x3[s][:, :], pL2[s][:, :], x2s[s][:, :], ALU.add).then_inc(c_x3, 1)

                def x3_low(p, s):
                    dve.wait_ge(c_x3h, p + 1)
                    nc.vector.tensor_tensor(x3s[s][:, 1, :], x3[s][:, :], x3s[s][:, 0, :].bitcast(f32),
                                            ALU.subtract).then_inc(c_x3l, 1)

                def y_sum(p, s, n):
                    dve.wait_ge(c_l3, p + 1)
                    if not isinstance(p, int) or p >= 2:
                        dve.wait_ge(c_out[s], 16 * n)
                    nc.vector.tensor_tensor(y[s][:, :], pL3[s][:, :], x3[s][:, :], ALU.add).then_inc(c_y, 1)

                xt_low(0, 0)
                w3_low(0, 0)
                xt_low(1, 1)
                w3_low(1, 1)
                u_mask(0, 0)
                x3_sum(0, 0)
                def pairs(i):
                    for s in range(2):
                        p = 2 * i + s
                        xt_low(p, s)
                        x3_low(p - 2, s)
                        w3_low(p, s)
                        u_mask(p - 1, 1 - s)
                        y_sum(p - 2, s, i - 1)
                        x3_sum(p - 1, 1 - s)

                pairs(1)
                with dve.Fori(2, PAIRS // 2) as i:
                    pairs(i)
                x3_low(PAIRS - 2, 0)
                u_mask(PAIRS - 1, 1)
                y_sum(PAIRS - 2, 0, PAIRS // 2 - 1)
                x3_sum(PAIRS - 1, 1)
                x3_low(PAIRS - 1, 1)
                y_sum(PAIRS - 1, 1, PAIRS // 2 - 1)

            @block.tensor
            def _(pe):
                pe.wait_ge(c_tab, 16 * (2 + ADAPTERS))
                for n in range(TABS):
                    for k in range(KT):
                        src = (w2_raw[:, k, n * P:(n + 1) * P] if n < KT else
                               a2_raw[:, k * P:(k + 1) * P] if n == KT else b2_raw[:, k, :])
                        last = nc.tensor.transpose(bank[n][:, k * P:(k + 1) * P], src, ident[:, :])
                    last.then_inc(c_tt, 1)

                def transposes(p, s, n):
                    pe.wait_ge(c_x2[s], 16 * (n + 1))
                    if not isinstance(p, int) or p >= 2:
                        pe.wait_ge(c_xl, p - 1)
                    for k in range(KT):
                        last = nc.tensor.transpose(pT[s][:, k * P:(k + 1) * P], x2s[s][:, k * P:(k + 1) * P], ident[:, :])
                    last.then_inc(c_tr, 1)

                def lora_in(p, s):
                    pe.wait_ge(c_xl, p + 1)
                    if not isinstance(p, int) or p >= 2:
                        pe.wait_ge(c_um, p - 1)
                    for k in range(KT):
                        for n, (a, b) in enumerate(((0, 0), (0, 1), (1, 0))):
                            last = nc.tensor.matmul(pU[s][:, 0:P], A2T[:, a, k, :], x2t[s][:, b, k, :],
                                                    start=(k == 0 and n == 0), stop=(k == KT - 1 and n == 2))
                    last.then_inc(c_u, 1)

                def layer2(p, s):
                    if not isinstance(p, int) or p >= 2:
                        pe.wait_ge(c_x3, p - 1)
                    for k in range(KT):
                        for n, (a, b) in enumerate(((0, 0), (0, 1), (1, 0))):
                            nc.tensor.matmul(pL2[s][:, :], x2t[s][:, a, k, :], W2T[:, b, k, :],
                                             start=(k == 0 and n == 0), stop=False)

                def lora_out(p, s):
                    pe.wait_ge(c_ul, p + 1)
                    for n, (a, b) in enumerate(((0, 0), (0, 1), (1, 0))):
                        last = nc.tensor.matmul(pL2[s][:, :], u2s[s][:, a, :], B2T[:, b, :], start=False, stop=(n == 2))
                    last.then_inc(c_l2, 1)

                def layer3(p, s):
                    pe.wait_ge(c_x3l, p + 1)
                    pe.wait_ge(c_w3l, p + 1)
                    if not isinstance(p, int) or p >= 2:
                        pe.wait_ge(c_y, p - 1)
                    for n, (a, b) in enumerate(((0, 0), (0, 1), (1, 0))):
                        last = nc.tensor.matmul(pL3[s][:, :], w3bd[s][:, a, :], x3s[s][:, b, :], start=(n == 0), stop=(n == 2))
                    last.then_inc(c_l3, 1)

                pe.wait_ge(c_tl, TABS)
                transposes(0, 0, 0)
                transposes(1, 1, 0)
                lora_in(0, 0)
                layer2(0, 0)
                lora_out(0, 0)
                def pairs(i):
                    for s in range(2):
                        p = 2 * i + s
                        transposes(p, s, i)
                        lora_in(p - 1, 1 - s)
                        layer2(p - 1, 1 - s)
                        layer3(p - 2, s)
                        lora_out(p - 1, 1 - s)

                pairs(1)
                with pe.Fori(2, PAIRS // 2) as i:
                    pairs(i)
                lora_in(PAIRS - 1, 1)
                layer2(PAIRS - 1, 1)
                layer3(PAIRS - 2, 0)
                lora_out(PAIRS - 1, 1)
                layer3(PAIRS - 1, 1)


_INS = ['x', 'itok_B_0_7', 'fside_8xS_0', 'itok_B_0_6', 'itok_B_1_198', 'L0_cond_weights', 'L1_cond_Wg', 'L1_cond_Wu',
        'L1_cond_Wd', 'L1_cond_Ag', 'L1_cond_Bg', 'L1_cond_Au', 'L1_cond_Bu', 'L1_cond_Ad', 'L1_cond_Bd', 'L2_cond_W',
        'L2_cond_A', 'L2_cond_Bm', 'L2_cond_scalings', 'L3_cond_weights']
_OUTS = [((32, 64, 512), 'float32')]


def kernel(**inputs):
    import numpy as _np
    import concourse.bacc as _bacc
    from concourse import mybir as _mybir
    from concourse.bass_utils import run_bass_kernel_spmd as _run

    nc = _bacc.Bacc("TRN2", target_bir_lowering=False, num_devices=1, dynamic_dma_scratch_size=4096)
    arrays, args = {}, []
    for name in _INS:
        a = _np.ascontiguousarray(inputs[name])
        arrays[f"in_{name}_dram"] = a
        args.append(nc.dram_tensor(f"in_{name}_dram", a.shape, _mybir.dt.from_np(a.dtype), kind="ExternalInput").ap())
    for i, (shape, dtype) in enumerate(_OUTS):
        dt = _mybir.dt.from_np(_np.dtype(dtype))
        args.append(nc.dram_tensor(f"out_{i}_dram", shape, dt, kind="ExternalOutput").ap())
    conditioned_residual_stack(nc, *args)
    r = _run(nc, [arrays], core_ids=[0])
    return r.results[0]["out_0_dram"]
```

```python
import concourse.bass as bass
from concourse import mybir
from contextlib import ExitStack



def conditioned_residual_stack(nc, x, idx_a, bias0, idx_b, idx_c, w0, wg, wu, wd, ag, bg, au, bu, ad, bd,
                               w2, a2, b2, scal2, w3, out):
    f32, r32, i32 = mybir.dt.float32, mybir.dt.float32r, mybir.dt.int32
    u32 = mybir.dt.uint32
    ALU = mybir.AluOpType
    ACT = mybir.ActivationFunctionType
    X = mybir.AxisListType.X

    SAMPLES, POS, FEAT = x.shape
    HIDDEN = wg.shape[1]
    ADAPTERS, _, RANK = ag.shape
    P = 128
    PAIRS = SAMPLES // 2
    GP = 4
    GROUPS = PAIRS // GP
    TOK = GP * P
    KT = FEAT // P
    FT = HIDDEN // P
    SLOTS = ADAPTERS * RANK
    T = GROUPS * FT
    assert SLOTS == P and 2 * POS == P

    x_pairs = x.rearrange("b c t -> (b c) t")
    out_pairs = out.rearrange("b c t -> (b c) t")
    bg_rows = bg.rearrange("n r f -> (n r) f")
    bu_rows = bu.rearrange("n r f -> (n r) f")

    ds, ts = bass.ds, bass.ts

    ctx = ExitStack()
    with ctx:
        def sb(name, shape, dt=f32, stack=ctx):
            return stack.enter_context(nc.sbuf_tensor(name, shape, dt))

        def sem(name):
            return ctx.enter_context(nc.semaphore(name))

        bank = [ctx.enter_context(nc.psum_tensor(f"bank{i}", [P, 512], f32)) for i in range(8)]

        X1 = sb("X1", [P, PAIRS, FEAT])
        ident = sb("ident", [P, P])
        mask1 = sb("mask1", [P, SAMPLES])
        mask2 = sb("mask2", [P, SAMPLES])
        w3raw = sb("w3raw", [P, PAIRS, POS])

        main = ExitStack()
        ctx.enter_context(main)
        XT = sb("XT", [P, 2, KT, PAIRS * P], r32, main)
        UT = sb("UT", [P, 2, 2, PAIRS * P], r32, main)
        ad_raw = sb("ad_raw", [P, FT, SLOTS], f32, main)
        BDS = sb("BDS", [P, 2, FEAT], r32, main)

        pa = ExitStack()
        idx = sb("idx", [P, 3, SAMPLES], i32, pa)
        idxf = sb("idxf", [P, 3, SAMPLES], f32, pa)
        row_i = sb("row_i", [P, 2], i32, pa)
        row_n = sb("row_n", [P, 1], f32, pa)
        lane = sb("lane", [P, PAIRS], i32, pa)
        offs = sb("offs", [P, 2, PAIRS], i32, pa)
        scal = sb("scal", [P, ADAPTERS], f32, pa)
        srow = sb("srow", [P, 1], f32, pa)
        biasT = sb("biasT", [P, ADAPTERS], f32, pa)
        napt = sb("napt", [P, ADAPTERS], i32, pa)
        naptf = sb("naptf", [P, ADAPTERS], f32, pa)
        beq = sb("beq", [P, PAIRS, ADAPTERS], f32, pa)
        bias = sb("bias", [P, PAIRS], f32, pa)
        agu_raw = sb("agu_raw", [P, 2, KT, SLOTS], f32, pa)
        AGU = sb("AGU", [P, 2, 2, KT, SLOTS], r32, pa)
        bd_raw = sb("bd_raw", [P, FEAT], f32, pa)
        w0raw = sb("w0raw", [P, PAIRS, POS], f32, pa)
        w0bd = [sb(f"w0bd{s}", [P, 2, P], r32, pa) for s in range(2)]
        xs = [sb(f"xs{s}", [P, FEAT], f32, pa) for s in range(2)]
        xh = [sb(f"xh{s}", [P, 2, FEAT], r32, pa) for s in range(2)]
        x1s = [sb(f"x1s{s}", [P, FEAT], f32, pa) for s in range(2)]
        ut = [sb(f"ut{j}", [P, TOK], f32, pa) for j in range(2)]

        s_idx, s_small, s_tab, s_tab2, s_dch, s_pch = (sem(n) for n in
            ("s_idx", "s_small", "s_tab", "s_tab2", "s_dch", "s_pch"))
        s_consts, s_ident, s_offs = sem("s_consts"), sem("s_ident"), sem("s_offs")
        s_zero, s_tabh, s_tabl = sem("s_zero"), sem("s_tabh"), sem("s_tabl")
        s_xload = [sem(f"s_xload{s}") for s in range(2)]
        s_xkept = [sem(f"s_xkept{s}") for s in range(2)]
        s_w0 = [sem(f"s_w0_{s}") for s in range(2)]
        s_w3 = sem("s_w3")
        s_xh, s_w0h, s_xsplit, s_l0, s_x1 = sem("s_xh"), sem("s_w0h"), sem("s_xsplit"), sem("s_l0"), sem("s_x1")
        s_tr, s_xth, s_xtl, s_u, s_um, s_uh, s_ul = (sem(n) for n in
            ("s_tr", "s_xth", "s_xtl", "s_u", "s_um", "s_uh", "s_ul"))

        psL0, psT, psU = bank[0:2], bank[2:4], bank[4:6]

        def later(n, least):
            return not isinstance(n, int) or n >= least

        with nc.Block() as block:

            @block.sync
            def _(sp):
                for n, v in enumerate((idx_a, idx_b, idx_c)):
                    sp.dma_start(idx[:, n, :], v.partition_broadcast(P)).then_inc(s_idx, 16)
                for s in range(2):
                    sp.dma_start(xs[s][:, :], x_pairs[s * P:(s + 1) * P, :]).then_inc(s_xload[s], 16)

                def keep(p, s):
                    sp.wait_ge(s_x1, p + 1)
                    sp.dma_start(X1[:, ds(p, 1), :], x1s[s][:, :]).then_inc(s_xkept[s], 16)

                def load(p, s):
                    sp.dma_start(xs[s][:, :], x_pairs[ds(p * P, P), :]).then_inc(s_xload[s], 16)

                with sp.Fori(0, PAIRS // 2 - 1) as i:
                    for s in range(2):
                        keep(2 * i + s, s)
                        load(2 * i + s + 2, s)
                for s in range(2):
                    keep(PAIRS - 2 + s, s)
                for s in range(2):
                    sp.wait_ge(s_xkept[s], 16 * PAIRS // 2)

            @block.gpsimd
            def _(pool):
                nc.gpsimd.iota(row_i[:, 0:1], [[0, 1]], base=0, channel_multiplier=1).then_inc(s_consts, 1)
                nc.gpsimd.iota(lane[:, :], [[0, PAIRS]], base=0, channel_multiplier=1).then_inc(s_consts, 1)
                nc.gpsimd.iota(napt[:, :], [[1, ADAPTERS]], base=0, channel_multiplier=0).then_inc(s_consts, 1)
                nc.gpsimd.memset(ident[:, :], 0.0).then_inc(s_pch, 1)
                pool.wait_ge(s_pch, 1)
                nc.gpsimd.affine_select(out=ident[:, :], in_=ident[:, :], compare_op=ALU.not_equal, fill=1.0, base=0,
                                        pattern=[[-1, P]], channel_multiplier=1).then_inc(s_ident, 1)
                pool.wait_ge(s_offs, 2)
                rows0 = w0.rearrange("n c d -> (n c) d")
                rows3 = w3.rearrange("n c d -> (n c) d")
                for p in range(PAIRS):
                    s = p % 2
                    if p >= 2:
                        pool.wait_ge(s_w0[s], 16 * (p // 2))
                    nc.gpsimd.indirect_dma_start(
                        w0raw[:, p, :], None, rows0,
                        bass.IndirectOffsetOnAxis(offs[:, 0, p:p + 1].bitcast(u32), 0)).then_inc(s_w0[s], 16)
                for p in range(PAIRS):
                    nc.gpsimd.indirect_dma_start(
                        w3raw[:, p, :], None, rows3,
                        bass.IndirectOffsetOnAxis(offs[:, 1, p:p + 1].bitcast(u32), 0)).then_inc(s_w3, 16)
                pool.wait_ge(s_w3, 16 * PAIRS)

            @block.scalar
            def _(act):
                act.dma_start(scal[:, :], scal2.partition_broadcast(P)).then_inc(s_small, 16)
                with nc.allow_non_contiguous_dma(reason="512 values, once"):
                    for s in range(2):
                        act.dma_start(biasT[s * POS:(s + 1) * POS, :], bias0.rearrange("n d -> d n")).then_inc(s_small, 16)
                for j, a in enumerate((ag, au)):
                    for k in range(KT):
                        act.dma_start(agu_raw[:, j, k, :].rearrange("p (n r) -> p n r", n=ADAPTERS),
                                      a[:, k * P:(k + 1) * P, :].rearrange("n p r -> p n r")).then_inc(s_tab, 16)

                def x_high(p, s, n):
                    act.wait_ge(s_xload[s], 16 * (n + 1))
                    if later(p, 2):
                        act.wait_ge(s_l0, p - 1)
                    nc.scalar.activation(xh[s][:, 0, :], xs[s][:, :], ACT.Copy).then_inc(s_xh, 1)
                    act.wait_ge(s_w0[s], 16 * (n + 1))
                    for h in range(2):
                        last = nc.scalar.activation(w0bd[s][h * POS:(h + 1) * POS, 0, h * POS:(h + 1) * POS],
                                                    w0raw[h * POS:(h + 1) * POS, ds(p, 1), :], ACT.Copy)
                    last.then_inc(s_w0h, 1)

                def xt_high(p, s):
                    act.wait_ge(s_tr, p + 1)
                    nc.scalar.activation(XT[:, 0, :, ds(p * P, P)],
                                         psT[s][:, :].rearrange("p (k t) -> p k t", k=KT), ACT.Copy).then_inc(s_xth, 1)

                def u_high(g, j):
                    act.wait_ge(s_um, 2 * g + j + 1)
                    nc.scalar.activation(UT[:, j, 0, ds(g * TOK, TOK)], ut[j][:, :], ACT.Copy).then_inc(s_uh, 1)

                act.wait_ge(s_zero, 2)
                x_high(0, 0, 0)
                x_high(1, 1, 0)
                act.wait_ge(s_tab, 16 * 2 * KT)
                nc.scalar.activation(AGU[:, 0, :, :, :], agu_raw[:, :, :, :], ACT.Copy).then_inc(s_tabh, 1)
                x_high(2, 0, 1)
                xt_high(0, 0)
                x_high(3, 1, 1)
                xt_high(1, 1)
                for n in range(ADAPTERS):
                    act.dma_start(ad_raw[:, :, n * RANK:(n + 1) * RANK],
                                  ad[n].rearrange("(k p) r -> p k r", p=P)).then_inc(s_tab2, 16)
                act.dma_start(bd_raw[:, :], bd.rearrange("n r f -> (n r) f")).then_inc(s_tab2, 16)
                with act.Fori(1, GROUPS) as g:
                    for j in range(GP):
                        p = GP * g + j
                        x_high(p, j % 2, (GP // 2) * g + j // 2)
                        xt_high(p - 2, j % 2)
                        if j >= 2:
                            u_high(g - 1, j - 2)
                act.wait_ge(s_tab2, 16 * (ADAPTERS + 1))
                nc.scalar.activation(BDS[:, 0, :], bd_raw[:, :], ACT.Copy).then_inc(s_tabh, 1)
                xt_high(PAIRS - 2, 0)
                xt_high(PAIRS - 1, 1)
                u_high(GROUPS - 1, 0)
                u_high(GROUPS - 1, 1)

            @block.vector
            def _(dve):
                chain = [0]

                def link(ins):
                    chain[0] += 1
                    ins.then_inc(s_dch, 1)
                    dve.wait_ge(s_dch, chain[0])

                for s in range(2):
                    nc.vector.memset(w0bd[s][:, :, :].bitcast(f32), 0.0).then_inc(s_zero, 1)
                dve.wait_ge(s_consts, 3)
                dve.wait_ge(s_idx, 16 * 3)
                nc.vector.tensor_scalar(row_i[:, 1:2], row_i[:, 0:1], RANK.bit_length() - 1, None, ALU.logical_shift_right)
                for j, n in ((0, 0), (1, 2)):
                    for h in range(2):
                        rows = slice(h * POS, (h + 1) * POS)
                        nc.vector.tensor_scalar(offs[rows, j, :], idx[rows, n, :].rearrange("p (q h) -> p q h", h=2)[:, :, h],
                                                POS.bit_length() - 1, None, ALU.logical_shift_left)
                link(nc.vector.tensor_scalar(lane[:, :], lane[:, :], POS - 1, None, ALU.bitwise_and))
                for j in range(2):
                    nc.vector.tensor_tensor(offs[:, j, :], offs[:, j, :], lane[:, :], ALU.add).then_inc(s_offs, 1)
                nc.vector.tensor_copy(row_n[:, :], row_i[:, 1:2])
                nc.vector.tensor_copy(idxf[:, :, :], idx[:, :, :])
                link(nc.vector.tensor_copy(naptf[:, :], napt[:, :]))

                def bias_and_masks():
                    dve.wait_ge(s_small, 16 * 3)
                    for h in range(2):
                        rows = slice(h * POS, (h + 1) * POS)
                        sel = idxf[rows, 0, :].rearrange("p (q h) -> p q h", h=2)[:, :, h:h + 1]
                        link(nc.vector.tensor_tensor(beq[rows, :, :], sel.to_broadcast([POS, PAIRS, ADAPTERS]),
                                                     naptf[rows, :].unsqueeze(1).to_broadcast([POS, PAIRS, ADAPTERS]),
                                                     ALU.is_equal))
                    link(nc.vector.tensor_tensor(beq[:, :, :], beq[:, :, :],
                                                 biasT[:, :].unsqueeze(1).to_broadcast([P, PAIRS, ADAPTERS]), ALU.mult))
                    link(nc.vector.tensor_reduce(bias[:, :], beq[:, :, :], X, ALU.add))
                    link(nc.vector.tensor_scalar(naptf[:, :], naptf[:, :], row_n[:, 0:1], None, ALU.is_equal))
                    link(nc.vector.tensor_tensor(naptf[:, :], naptf[:, :], scal[:, :], ALU.mult))
                    link(nc.vector.tensor_reduce(srow[:, :], naptf[:, :], X, ALU.add))
                    nc.vector.tensor_scalar(mask1[:, :], idxf[:, 0, :], row_n[:, 0:1], None, ALU.is_equal)
                    link(nc.vector.tensor_scalar(mask2[:, :], idxf[:, 1, :], row_n[:, 0:1], srow[:, 0:1],
                                                 ALU.is_equal, ALU.mult))

                def x_low(p, s):
                    dve.wait_ge(s_xh, p + 1)
                    nc.vector.tensor_tensor(xh[s][:, 1, :], xs[s][:, :], xh[s][:, 0, :].bitcast(f32), ALU.subtract)
                    dve.wait_ge(s_w0h, p + 1)
                    for h in range(2):
                        rows = slice(h * POS, (h + 1) * POS)
                        last = nc.vector.tensor_tensor(w0bd[s][rows, 1, rows], w0raw[rows, ds(p, 1), :].rearrange("p a d -> p (a d)"),
                                                       w0bd[s][rows, 0, rows].bitcast(f32), ALU.subtract)
                    last.then_inc(s_xsplit, 1)

                def x1(p, s, n):
                    dve.wait_ge(s_l0, p + 1)
                    if later(p, 2):
                        dve.wait_ge(s_tr, p - 1)
                        dve.wait_ge(s_xkept[s], 16 * n)
                    nc.vector.scalar_tensor_tensor(out=x1s[s][:, :], in0=psL0[s][:, :], scalar=bias[:, ds(p, 1)],
                                                   in1=xs[s][:, :], op0=ALU.add, op1=ALU.add).then_inc(s_x1, 1)

                def xt_low(p, s):
                    dve.wait_ge(s_xth, p + 1)
                    nc.vector.tensor_tensor(XT[:, 1, :, ds(p * P, P)],
                                            psT[s][:, :].rearrange("p (k t) -> p k t", k=KT),
                                            XT[:, 0, :, ds(p * P, P)].bitcast(f32), ALU.subtract).then_inc(s_xtl, 1)

                def u_mask(g, j):
                    dve.wait_ge(s_u, 2 * g + j + 1)
                    nc.vector.tensor_tensor(ut[j][:, :].rearrange("p (b t) -> p b t", t=POS),
                                            psU[j][:, :].rearrange("p (b t) -> p b t", t=POS),
                                            mask1[:, ds(2 * GP * g, 2 * GP)].unsqueeze(2).to_broadcast([P, 2 * GP, POS]),
                                            ALU.mult).then_inc(s_um, 1)

                def u_low(g, j):
                    dve.wait_ge(s_uh, 2 * g + j + 1)
                    nc.vector.tensor_tensor(UT[:, j, 1, ds(g * TOK, TOK)], ut[j][:, :],
                                            UT[:, j, 0, ds(g * TOK, TOK)].bitcast(f32), ALU.subtract).then_inc(s_ul, 1)

                bias_and_masks()
                x_low(0, 0)
                x_low(1, 1)
                x1(0, 0, 0)
                dve.wait_ge(s_tabh, 1)
                nc.vector.tensor_tensor(AGU[:, 1, :, :, :], agu_raw[:, :, :, :], AGU[:, 0, :, :, :].bitcast(f32),
                                        ALU.subtract).then_inc(s_tabl, 1)
                x_low(2, 0)
                x1(1, 1, 0)
                xt_low(0, 0)
                x_low(3, 1)
                x1(2, 0, 1)
                xt_low(1, 1)
                with dve.Fori(1, GROUPS) as g:
                    for j in range(GP):
                        p = GP * g + j
                        x_low(p, j % 2)
                        x1(p - 1, (j + 1) % 2, (GP // 2) * g + (j + 1) // 2 - 1)
                        xt_low(p - 2, j % 2)
                        if j >= 2:
                            u_mask(g - 1, j - 2)
                            u_low(g - 1, j - 2)
                x1(PAIRS - 1, 1, PAIRS // 2 - 1)
                dve.wait_ge(s_tabh, 2)
                nc.vector.tensor_tensor(BDS[:, 1, :], bd_raw[:, :], BDS[:, 0, :].bitcast(f32), ALU.subtract)
                xt_low(PAIRS - 2, 0)
                xt_low(PAIRS - 1, 1)
                for j in range(2):
                    u_mask(GROUPS - 1, j)
                    u_low(GROUPS - 1, j)

            @block.tensor
            def _(pe):
                def layer0(p, s):
                    pe.wait_ge(s_xsplit, p + 1)
                    if later(p, 2):
                        pe.wait_ge(s_x1, p - 1)
                    for n, (a, b) in enumerate(((0, 0), (0, 1), (1, 0))):
                        last = nc.tensor.matmul(psL0[s][:, :], w0bd[s][:, a, :], xh[s][:, b, :], start=(n == 0), stop=(n == 2))
                    last.then_inc(s_l0, 1)

                def transposes(p, s):
                    pe.wait_ge(s_x1, p + 1)
                    if later(p, 2):
                        pe.wait_ge(s_xtl, p - 1)
                    for k in range(KT):
                        last = nc.tensor.transpose(psT[s][:, k * P:(k + 1) * P], x1s[s][:, k * P:(k + 1) * P], ident[:, :])
                    last.then_inc(s_tr, 1)

                def lora_in(g, j):
                    pe.wait_ge(s_xtl, GP * g + GP)
                    if later(g, 1):
                        pe.wait_ge(s_um, 2 * g + j - 1)
                    for k in range(KT):
                        for n, (a, b) in enumerate(((0, 0), (0, 1), (1, 0))):
                            last = nc.tensor.matmul(psU[j][:, :], AGU[:, a, j, k, :], XT[:, b, k, ds(g * TOK, TOK)],
                                                    start=(k == 0 and n == 0), stop=(k == KT - 1 and n == 2))
                    last.then_inc(s_u, 1)

                layer0(0, 0)
                pe.wait_ge(s_ident, 1)
                for p in range(1, GP):
                    layer0(p, p % 2)
                    transposes(p - 1, (p - 1) % 2)
                pe.wait_ge(s_tabl, 1)

                def group(g):
                    for j in range(GP):
                        p = GP * g + j
                        layer0(p, j % 2)
                        transposes(p - 1, (j + 1) % 2)
                        if j >= 2:
                            lora_in(g - 1, j - 2)

                group(1)
                with pe.Fori(2, GROUPS) as g:
                    group(g)
                transposes(PAIRS - 1, 1)
                lora_in(GROUPS - 1, 0)
                lora_in(GROUPS - 1, 1)

        pa.close()

        GU = 2 * (KT + 1) * P
        DN = FEAT + SLOTS
        stage = [sb(f"stage{s}", [P, GU + DN], f32, main) for s in range(2)]
        gu = [sb(f"gu{s}", [P, 2, 2, KT + 1, P], r32, main) for s in range(2)]
        wds = [sb(f"wds{s}", [P, 2, DN], r32, main) for s in range(2)]
        hid = [sb(f"hid{s}", [P, TOK], f32, main) for s in range(2)]
        hs = [sb(f"hs{s}", [P, 2, TOK], r32, main) for s in range(2)]
        udc = sb("udc", [P, TOK], f32, main)
        uds = sb("uds", [P, 2, TOK], r32, main)

        psG, psUp, psD, psUd = bank[0], bank[1], bank[2:6], bank[6]

        s_wload = [sem(f"s_wload{s}") for s in range(2)]
        s_guh, s_gul, s_wdh, s_wdl = sem("s_guh"), sem("s_gul"), sem("s_wdh"), sem("s_wdl")
        s_gate, s_silu, s_up, s_hid, s_hh, s_hl, s_down = (sem(n) for n in
            ("s_gate", "s_silu", "s_up", "s_hid", "s_hh", "s_hl", "s_down"))
        s_udm, s_udh, s_udl, s_lb, s_x2 = (sem(n) for n in ("s_udm", "s_udh", "s_udl", "s_lb", "s_x2"))
        DMAS = 6

        with nc.Block() as block:

            @block.sync
            def _(sp):
                def load(f, s):
                    g2 = stage[s][:, 0:GU].rearrange("p (j k f) -> p j k f", j=2, k=KT + 1)
                    cols = ds(f * P, P)
                    for j, (w, b) in enumerate(((wg, bg_rows), (wu, bu_rows))):
                        sp.dma_start(g2[:, j, 0:KT, :], w.rearrange("(k p) f -> p k f", p=P)[:, :, cols]).then_inc(s_wload[s], 16)
                        sp.dma_start(g2[:, j, KT, :], b[:, cols]).then_inc(s_wload[s], 16)
                    sp.dma_start(stage[s][:, GU:GU + FEAT], wd[cols, :]).then_inc(s_wload[s], 16)
                    sp.dma_start(stage[s][:, GU + FEAT:GU + DN], ad_raw[:, ds(f, 1), :]).then_inc(s_wload[s], 16)

                load(0, 0)
                load(1, 1)
                with sp.Fori(1, FT // 2) as i:
                    for s in range(2):
                        sp.wait_ge(s_wdl, 2 * i + s - 1)
                        sp.wait_ge(s_gul, 2 * i + s - 1)
                        load(2 * i + s, s)
                with sp.Fori(1, GROUPS) as g:
                    with sp.Fori(0, FT // 2) as i:
                        for s in range(2):
                            sp.wait_ge(s_wdl, FT * g + 2 * i + s - 1)
                            sp.wait_ge(s_gul, FT * g + 2 * i + s - 1)
                            load(2 * i + s, s)

            @block.scalar
            def _(act):
                def gu_high(t, s, n):
                    act.wait_ge(s_wload[s], 16 * DMAS * (n + 1))
                    if later(t, 2):
                        act.wait_ge(s_up, t - 1)
                    nc.scalar.activation(gu[s][:, 0, :, :, :].rearrange("p j k f -> p (j k f)"),
                                         stage[s][:, 0:GU], ACT.Copy).then_inc(s_guh, 1)

                def wd_high(t, s):
                    if later(t, 2):
                        act.wait_ge(s_down, t - 1)
                    nc.scalar.activation(wds[s][:, 0, :], stage[s][:, GU:GU + DN], ACT.Copy).then_inc(s_wdh, 1)

                def silu(t, s):
                    act.wait_ge(s_gate, t + 1)
                    if later(t, 2):
                        act.wait_ge(s_hl, t - 1)
                    nc.scalar.activation(hid[s][:, :], psG[:, :], ACT.Silu).then_inc(s_silu, 1)

                def hid_high(t, s):
                    act.wait_ge(s_hid, t + 1)
                    if later(t, 2):
                        act.wait_ge(s_down, t - 1)
                    nc.scalar.activation(hs[s][:, 0, :], hid[s][:, :], ACT.Copy).then_inc(s_hh, 1)

                def step(t, s, n):
                    gu_high(t, s, n)
                    wd_high(t - 1, 1 - s)
                    silu(t - 1, 1 - s)

                def ud_high(g):
                    act.wait_ge(s_udm, g + 1)
                    if later(g, 1):
                        act.wait_ge(s_lb, g)
                    nc.scalar.activation(uds[:, 0, :], udc[:, :], ACT.Copy).then_inc(s_udh, 1)

                def inner(t0, n0):
                    with act.Fori(1, FT // 2) as i:
                        for s in range(2):
                            step(t0 + 2 * i + s, s, n0 + i)
                            hid_high(t0 + 2 * i + s - 1, 1 - s)

                gu_high(0, 0, 0)
                step(1, 1, 0)
                hid_high(0, 0)
                inner(0, 0)
                with act.Fori(1, GROUPS) as g:
                    t0, n0 = FT * g, FT // 2 * g
                    step(t0, 0, n0)
                    hid_high(t0 - 1, 1)
                    ud_high(g - 1)
                    step(t0 + 1, 1, n0)
                    hid_high(t0, 0)
                    inner(t0, n0)
                wd_high(T - 1, 1)
                silu(T - 1, 1)
                hid_high(T - 1, 1)
                ud_high(GROUPS - 1)

            @block.vector
            def _(dve):
                def gu_low(t, s):
                    dve.wait_ge(s_guh, t + 1)
                    nc.vector.tensor_tensor(gu[s][:, 1, :, :, :].rearrange("p j k f -> p (j k f)"), stage[s][:, 0:GU],
                                            gu[s][:, 0, :, :, :].rearrange("p j k f -> p (j k f)").bitcast(f32),
                                            ALU.subtract).then_inc(s_gul, 1)

                def wd_low(t, s):
                    dve.wait_ge(s_wdh, t + 1)
                    nc.vector.tensor_tensor(wds[s][:, 1, :], stage[s][:, GU:GU + DN], wds[s][:, 0, :].bitcast(f32),
                                            ALU.subtract).then_inc(s_wdl, 1)

                def gated(t, s):
                    dve.wait_ge(s_up, t + 1)
                    dve.wait_ge(s_silu, t + 1)
                    nc.vector.tensor_tensor(hid[s][:, :], psUp[:, :], hid[s][:, :], ALU.mult).then_inc(s_hid, 1)

                def hid_low(t, s):
                    dve.wait_ge(s_hh, t + 1)
                    nc.vector.tensor_tensor(hs[s][:, 1, :], hid[s][:, :], hs[s][:, 0, :].bitcast(f32),
                                            ALU.subtract).then_inc(s_hl, 1)

                def ud_mask(g):
                    dve.wait_ge(s_down, FT * g + FT)
                    nc.vector.tensor_tensor(udc[:, :].rearrange("p (b t) -> p b t", t=POS),
                                            psUd[:, :].rearrange("p (b t) -> p b t", t=POS),
                                            mask1[:, ds(2 * GP * g, 2 * GP)].unsqueeze(2).to_broadcast([P, 2 * GP, POS]),
                                            ALU.mult).then_inc(s_udm, 1)
                    dve.wait_ge(s_udh, g + 1)
                    nc.vector.tensor_tensor(uds[:, 1, :], udc[:, :], uds[:, 0, :].bitcast(f32),
                                            ALU.subtract).then_inc(s_udl, 1)

                def x2(g):
                    dve.wait_ge(s_lb, g + 1)
                    for j in range(GP):
                        dst = X1[:, ds(GP * g + j, 1), :].rearrange("p a f -> p (a f)")
                        last = nc.vector.tensor_tensor(dst, psD[j][:, :], dst, ALU.add)
                    last.then_inc(s_x2, 1)

                def step(t, s):
                    gu_low(t, s)
                    wd_low(t - 1, 1 - s)
                    gated(t - 1, 1 - s)
                    hid_low(t - 1, 1 - s)

                def inner(t0):
                    with dve.Fori(1, FT // 2) as i:
                        for s in range(2):
                            step(t0 + 2 * i + s, s)

                gu_low(0, 0)
                step(1, 1)
                inner(0)
                with dve.Fori(1, GROUPS) as g:
                    step(FT * g, 0)
                    ud_mask(g - 1)
                    step(FT * g + 1, 1)
                    x2(g - 1)
                    inner(FT * g)
                wd_low(T - 1, 1)
                gated(T - 1, 1)
                hid_low(T - 1, 1)
                ud_mask(GROUPS - 1)
                x2(GROUPS - 1)

            @block.tensor
            def _(pe):
                def half(j, t, s, g, psum, done):
                    for k in range(KT + 1):
                        for n, (a, b) in enumerate(((0, 0), (0, 1), (1, 0))):
                            src = XT[:, b, k, ds(g * TOK, TOK)] if k < KT else UT[:, j, b, ds(g * TOK, TOK)]
                            last = nc.tensor.matmul(psum[:, :], gu[s][:, a, j, k, :], src,
                                                    start=(k == 0 and n == 0), stop=(k == KT and n == 2))
                    last.then_inc(done, 1)

                def gate(t, s, g):
                    pe.wait_ge(s_gul, t + 1)
                    if later(t, 1):
                        pe.wait_ge(s_silu, t)
                    half(0, t, s, g, psG, s_gate)

                def up(t, s, g):
                    if later(t, 1):
                        pe.wait_ge(s_hid, t)
                    half(1, t, s, g, psUp, s_up)

                def down(t, s, first=False, final=False):
                    pe.wait_ge(s_hl, t + 1)
                    pe.wait_ge(s_wdl, t + 1)
                    for j in range(GP):
                        for n, (a, b) in enumerate(((0, 0), (0, 1), (1, 0))):
                            nc.tensor.matmul(psD[j][:, :], hs[s][:, a, j * P:(j + 1) * P], wds[s][:, b, 0:FEAT],
                                             start=(first and n == 0), stop=False)
                    for n, (a, b) in enumerate(((0, 0), (0, 1), (1, 0))):
                        last = nc.tensor.matmul(psUd[:, :], wds[s][:, a, FEAT:DN], hs[s][:, b, :],
                                                start=(first and n == 0), stop=(final and n == 2))
                    last.then_inc(s_down, 1)

                def lora_down(g):
                    pe.wait_ge(s_udl, g + 1)
                    for j in range(GP):
                        for n, (a, b) in enumerate(((0, 0), (0, 1), (1, 0))):
                            last = nc.tensor.matmul(psD[j][:, :], uds[:, a, j * P:(j + 1) * P], BDS[:, b, :],
                                                    start=False, stop=(n == 2))
                    last.then_inc(s_lb, 1)

                def inner(t0, g):
                    with pe.Fori(1, FT // 2) as i:
                        for s in range(2):
                            t = t0 + 2 * i + s
                            gate(t, s, g)
                            up(t, s, g)
                            down(t - 1, 1 - s)

                gate(0, 0, 0)
                up(0, 0, 0)
                gate(1, 1, 0)
                up(1, 1, 0)
                down(0, 0, first=True)
                inner(0, 0)
                with pe.Fori(1, GROUPS) as g:
                    t0 = FT * g
                    gate(t0, 0, g)
                    down(t0 - 1, 1, final=True)
                    up(t0, 0, g)
                    gate(t0 + 1, 1, g)
                    lora_down(g - 1)
                    up(t0 + 1, 1, g)
                    pe.wait_ge(s_x2, g)
                    down(t0, 0, first=True)
                    inner(t0, g)
                down(T - 1, 1, final=True)
                lora_down(GROUPS - 1)

        main.close()

        DUO = 2 * P
        DUOS = PAIRS // 2
        w2_raw = sb("w2_raw", [P, KT, FEAT])
        a2_raw = sb("a2_raw", [P, FEAT])
        b2_raw = sb("b2_raw", [P, KT, SLOTS])
        W2T = sb("W2T", [P, 2, KT, FEAT], r32)
        A2T = sb("A2T", [P, 2, KT, SLOTS], r32)
        B2T = sb("B2T", [P, 2, FEAT], r32)
        x2s = [sb(f"x2s{s}", [P, 2, FEAT]) for s in range(2)]
        x2t = [sb(f"x2t{s}", [P, 2, KT, DUO], r32) for s in range(2)]
        u2 = sb("u2", [P, DUO])
        u2s = sb("u2s", [P, 2, DUO], r32)
        x3 = [[sb(f"x3_{s}_{q}", [P, FEAT]) for q in range(2)] for s in range(2)]
        x3s = [sb(f"x3s{q}", [P, 2, FEAT], r32) for q in range(2)]
        w3bd = [sb(f"w3bd{q}", [P, 2, P], r32) for q in range(2)]
        y = [sb(f"y{q}", [P, FEAT]) for q in range(2)]

        pT, pU, pL2, pL3 = bank[0:2], bank[2], bank[3:5], bank[5:7]
        c_tab = sem("c_tab")
        c_tt, c_th, c_tl, c_zero = sem("c_tt"), sem("c_th"), sem("c_tl"), sem("c_zero")
        c_x2 = [sem(f"c_x2_{s}") for s in range(2)]
        c_out = [sem(f"c_out{q}") for q in range(2)]
        c_tr, c_xh, c_xl, c_u, c_um, c_uh, c_ul, c_l2, c_x3, c_x3h, c_x3l, c_w3h, c_w3l, c_l3, c_y = (sem(n) for n in
            ("c_tr", "c_xh", "c_xl", "c_u", "c_um", "c_uh", "c_ul", "c_l2", "c_x3", "c_x3h", "c_x3l", "c_w3h", "c_w3l",
             "c_l3", "c_y"))
        TABS = KT + 2

        with nc.Block() as block:

            @block.sync
            def _(sp):
                sp.dma_start(w2_raw[:, :, :], w2.rearrange("(k p) f -> p k f", p=P)).then_inc(c_tab, 16)

                def load(d, s):
                    sp.dma_start(x2s[s][:, :, :], X1[:, ds(2 * d, 2), :]).then_inc(c_x2[s], 16)

                def store(d):
                    for q in range(2):
                        sp.wait_ge(c_y, 2 * d + q + 1)
                        sp.dma_start(out_pairs[ds((2 * d + q) * P, P), :], y[q][:, :]).then_inc(c_out[q], 16)

                load(0, 0)
                load(1, 1)
                sp.wait_ge(c_x3, 2)
                load(2, 0)
                with sp.Fori(0, (DUOS - 4) // 2) as i:
                    for s in range(2):
                        d = 2 * i + s
                        store(d)
                        sp.wait_ge(c_x3, 2 * d + 4)
                        load(d + 3, 1 - s)
                store(DUOS - 4)
                sp.wait_ge(c_x3, 2 * DUOS - 4)
                load(DUOS - 1, 1)
                for d in range(DUOS - 3, DUOS):
                    store(d)
                for q in range(2):
                    sp.wait_ge(c_out[q], 16 * DUOS)

            @block.scalar
            def _(act):
                act.dma_start(a2_raw[:, :], a2.rearrange("n r f -> (n r) f")).then_inc(c_tab, 16)
                for k in range(KT):
                    act.dma_start(b2_raw[:, k, :].rearrange("p (n r) -> p n r", n=ADAPTERS),
                                  b2[:, k * P:(k + 1) * P, :].rearrange("n p r -> p n r")).then_inc(c_tab, 16)
                for n in range(TABS):
                    act.wait_ge(c_tt, n + 1)
                    dst = W2T[:, 0, n, :] if n < KT else A2T[:, 0, :, :].rearrange("p k f -> p (k f)") if n == KT else B2T[:, 0, :]
                    nc.scalar.activation(dst, bank[n][:, :], ACT.Copy).then_inc(c_th, 1)

                def xt_high(d, s):
                    for q in range(2):
                        act.wait_ge(c_tr, 2 * d + q + 1)
                        if later(d, 2) and q == 0:
                            act.wait_ge(c_l2, 2 * d - 2)
                        nc.scalar.activation(x2t[s][:, 0, :, q * P:(q + 1) * P],
                                             pT[q][:, :].rearrange("p (k t) -> p k t", k=KT), ACT.Copy).then_inc(c_xh, 1)

                def u_high(d):
                    act.wait_ge(c_um, d + 1)
                    if later(d, 1):
                        act.wait_ge(c_l2, 2 * d)
                    nc.scalar.activation(u2s[:, 0, :], u2[:, :], ACT.Copy).then_inc(c_uh, 1)

                def x3_high(d, s):
                    for q in range(2):
                        act.wait_ge(c_x3, 2 * d + q + 1)
                        if later(d, 1):
                            act.wait_ge(c_l3, 2 * d + q - 1)
                        nc.scalar.activation(x3s[q][:, 0, :], x3[s][q][:, :], ACT.Copy).then_inc(c_x3h, 1)
                        for h in range(2):
                            rows = slice(h * POS, (h + 1) * POS)
                            last = nc.scalar.activation(w3bd[q][rows, 0, rows], w3raw[rows, ds(2 * d + q, 1), :], ACT.Copy)
                        last.then_inc(c_w3h, 1)

                act.wait_ge(c_zero, 2)
                xt_high(0, 0)
                xt_high(1, 1)
                u_high(0)

                def duos(i):
                    for s in range(2):
                        d = 2 * i + s
                        x3_high(d - 2, s)
                        xt_high(d, s)
                        u_high(d - 1)

                duos(1)
                with act.Fori(2, DUOS // 2) as i:
                    duos(i)
                x3_high(DUOS - 2, 0)
                u_high(DUOS - 1)
                x3_high(DUOS - 1, 1)

            @block.vector
            def _(dve):
                for q in range(2):
                    nc.vector.memset(w3bd[q][:, :, :].bitcast(f32), 0.0).then_inc(c_zero, 1)
                for n in range(TABS):
                    dve.wait_ge(c_th, n + 1)
                    t = (W2T[:, :, n, :] if n < KT else A2T[:, :, :, :].rearrange("p a k f -> p a (k f)") if n == KT else B2T[:, :, :])
                    nc.vector.tensor_tensor(t[:, 1, :], bank[n][:, :], t[:, 0, :].bitcast(f32), ALU.subtract).then_inc(c_tl, 1)

                def xt_low(d, s):
                    for q in range(2):
                        dve.wait_ge(c_xh, 2 * d + q + 1)
                        nc.vector.tensor_tensor(x2t[s][:, 1, :, q * P:(q + 1) * P],
                                                pT[q][:, :].rearrange("p (k t) -> p k t", k=KT),
                                                x2t[s][:, 0, :, q * P:(q + 1) * P].bitcast(f32), ALU.subtract).then_inc(c_xl, 1)

                def u_mask(d):
                    dve.wait_ge(c_u, d + 1)
                    nc.vector.tensor_tensor(u2[:, :].rearrange("p (b t) -> p b t", t=POS),
                                            pU[:, 0:DUO].rearrange("p (b t) -> p b t", t=POS),
                                            mask2[:, ds(4 * d, 4)].unsqueeze(2).to_broadcast([P, 4, POS]),
                                            ALU.mult).then_inc(c_um, 1)
                    dve.wait_ge(c_uh, d + 1)
                    nc.vector.tensor_tensor(u2s[:, 1, :], u2[:, :], u2s[:, 0, :].bitcast(f32),
                                            ALU.subtract).then_inc(c_ul, 1)

                def x3_low(d, s):
                    for q in range(2):
                        dve.wait_ge(c_x3h, 2 * d + q + 1)
                        nc.vector.tensor_tensor(x3s[q][:, 1, :], x3[s][q][:, :], x3s[q][:, 0, :].bitcast(f32),
                                                ALU.subtract).then_inc(c_x3l, 1)
                        dve.wait_ge(c_w3h, 2 * d + q + 1)
                        for h in range(2):
                            rows = slice(h * POS, (h + 1) * POS)
                            last = nc.vector.tensor_tensor(w3bd[q][rows, 1, rows],
                                                           w3raw[rows, ds(2 * d + q, 1), :].rearrange("p a d -> p (a d)"),
                                                           w3bd[q][rows, 0, rows].bitcast(f32), ALU.subtract)
                        last.then_inc(c_w3l, 1)

                def x3_sum(d, s, q):
                    dve.wait_ge(c_l2, 2 * d + q + 1)
                    nc.vector.tensor_tensor(x3[s][q][:, :], pL2[q][:, :], x2s[s][:, q, :], ALU.add).then_inc(c_x3, 1)

                def y_sum(d, s, q):
                    dve.wait_ge(c_l3, 2 * d + q + 1)
                    if later(d, 1):
                        dve.wait_ge(c_out[q], 16 * d)
                    nc.vector.tensor_tensor(y[q][:, :], pL3[q][:, :], x3[s][q][:, :], ALU.add).then_inc(c_y, 1)

                xt_low(0, 0)
                xt_low(1, 1)
                u_mask(0)
                x3_sum(0, 0, 0)
                x3_sum(0, 0, 1)
                def duos(i):
                    for s in range(2):
                        d = 2 * i + s
                        x3_low(d - 2, s)
                        xt_low(d, s)
                        u_mask(d - 1)
                        for q in range(2):
                            y_sum(d - 2, s, q)
                            x3_sum(d - 1, 1 - s, q)

                duos(1)
                with dve.Fori(2, DUOS // 2) as i:
                    duos(i)
                x3_low(DUOS - 2, 0)
                u_mask(DUOS - 1)
                for q in range(2):
                    y_sum(DUOS - 2, 0, q)
                    x3_sum(DUOS - 1, 1, q)
                x3_low(DUOS - 1, 1)
                for q in range(2):
                    y_sum(DUOS - 1, 1, q)

            @block.tensor
            def _(pe):
                pe.wait_ge(c_tab, 16 * (2 + KT))
                for n in range(TABS):
                    for k in range(KT):
                        src = (w2_raw[:, k, n * P:(n + 1) * P] if n < KT else
                               a2_raw[:, k * P:(k + 1) * P] if n == KT else b2_raw[:, k, :])
                        last = nc.tensor.transpose(bank[n][:, k * P:(k + 1) * P], src, ident[:, :])
                    last.then_inc(c_tt, 1)

                def transposes(d, s, n):
                    pe.wait_ge(c_x2[s], 16 * (n + 1))
                    for q in range(2):
                        if later(d, 1):
                            pe.wait_ge(c_xl, 2 * d + q - 1)
                        for k in range(KT):
                            last = nc.tensor.transpose(pT[q][:, k * P:(k + 1) * P], x2s[s][:, q, k * P:(k + 1) * P], ident[:, :])
                        last.then_inc(c_tr, 1)

                def lora_in(d, s):
                    pe.wait_ge(c_xl, 2 * d + 2)
                    if later(d, 1):
                        pe.wait_ge(c_um, d)
                    for k in range(KT):
                        for n, (a, b) in enumerate(((0, 0), (0, 1), (1, 0))):
                            last = nc.tensor.matmul(pU[:, 0:DUO], A2T[:, a, k, :], x2t[s][:, b, k, :],
                                                    start=(k == 0 and n == 0), stop=(k == KT - 1 and n == 2))
                    last.then_inc(c_u, 1)

                def layer2(d, s, q):
                    if later(d, 1):
                        pe.wait_ge(c_x3, 2 * d + q - 1)
                    for k in range(KT):
                        for n, (a, b) in enumerate(((0, 0), (0, 1), (1, 0))):
                            nc.tensor.matmul(pL2[q][:, :], x2t[s][:, a, k, q * P:(q + 1) * P], W2T[:, b, k, :],
                                             start=(k == 0 and n == 0), stop=False)

                def lora_out(d, q):
                    pe.wait_ge(c_ul, d + 1)
                    for n, (a, b) in enumerate(((0, 0), (0, 1), (1, 0))):
                        last = nc.tensor.matmul(pL2[q][:, :], u2s[:, a, q * P:(q + 1) * P], B2T[:, b, :], start=False, stop=(n == 2))
                    last.then_inc(c_l2, 1)

                def layer3(d, q):
                    pe.wait_ge(c_x3l, 2 * d + q + 1)
                    pe.wait_ge(c_w3l, 2 * d + q + 1)
                    if later(d, 1):
                        pe.wait_ge(c_y, 2 * d + q - 1)
                    for n, (a, b) in enumerate(((0, 0), (0, 1), (1, 0))):
                        last = nc.tensor.matmul(pL3[q][:, :], w3bd[q][:, a, :], x3s[q][:, b, :], start=(n == 0), stop=(n == 2))
                    last.then_inc(c_l3, 1)

                pe.wait_ge(c_tl, TABS)
                transposes(0, 0, 0)
                transposes(1, 1, 0)
                lora_in(0, 0)
                for q in range(2):
                    layer2(0, 0, q)
                for q in range(2):
                    lora_out(0, q)

                def duos(i):
                    for s in range(2):
                        d = 2 * i + s
                        transposes(d, s, i)
                        lora_in(d - 1, 1 - s)
                        for q in range(2):
                            layer2(d - 1, 1 - s, q)
                        for q in range(2):
                            layer3(d - 2, q)
                            lora_out(d - 1, q)

                duos(1)
                with pe.Fori(2, DUOS // 2) as i:
                    duos(i)
                lora_in(DUOS - 1, 1)
                for q in range(2):
                    layer2(DUOS - 1, 1, q)
                for q in range(2):
                    layer3(DUOS - 2, q)
                    lora_out(DUOS - 1, q)
                for q in range(2):
                    layer3(DUOS - 1, q)


_INS = ['x', 'itok_B_0_7', 'fside_8xS_0', 'itok_B_0_6', 'itok_B_1_198', 'L0_cond_weights', 'L1_cond_Wg', 'L1_cond_Wu',
        'L1_cond_Wd', 'L1_cond_Ag', 'L1_cond_Bg', 'L1_cond_Au', 'L1_cond_Bu', 'L1_cond_Ad', 'L1_cond_Bd', 'L2_cond_W',
        'L2_cond_A', 'L2_cond_Bm', 'L2_cond_scalings', 'L3_cond_weights']
_OUTS = [((32, 64, 512), 'float32')]


def kernel(**inputs):
    import numpy as _np
    import concourse.bacc as _bacc
    from concourse import mybir as _mybir
    from concourse.bass_utils import run_bass_kernel_spmd as _run

    nc = _bacc.Bacc("TRN2", target_bir_lowering=False, num_devices=1, dynamic_dma_scratch_size=4096)
    arrays, args = {}, []
    for name in _INS:
        a = _np.ascontiguousarray(inputs[name])
        arrays[f"in_{name}_dram"] = a
        args.append(nc.dram_tensor(f"in_{name}_dram", a.shape, _mybir.dt.from_np(a.dtype), kind="ExternalInput").ap())
    for i, (shape, dtype) in enumerate(_OUTS):
        dt = _mybir.dt.from_np(_np.dtype(dtype))
        args.append(nc.dram_tensor(f"out_{i}_dram", shape, dt, kind="ExternalOutput").ap())
    conditioned_residual_stack(nc, *args)
    r = _run(nc, [arrays], core_ids=[0])
    return r.results[0]["out_0_dram"]
```

```python
import concourse.bass as bass
from concourse import mybir
from contextlib import ExitStack



def conditioned_residual_stack(nc, x, idx_a, bias0, idx_b, idx_c, w0, wg, wu, wd, ag, bg, au, bu, ad, bd,
                               w2, a2, b2, scal2, w3, out):
    f32, r32, i32 = mybir.dt.float32, mybir.dt.float32r, mybir.dt.int32
    u32 = mybir.dt.uint32
    ALU = mybir.AluOpType
    ACT = mybir.ActivationFunctionType
    X = mybir.AxisListType.X

    SAMPLES, POS, FEAT = x.shape
    HIDDEN = wg.shape[1]
    ADAPTERS, _, RANK = ag.shape
    P = 128
    PAIRS = SAMPLES // 2
    GP = 4
    GROUPS = PAIRS // GP
    TOK = GP * P
    KT = FEAT // P
    FT = HIDDEN // P
    SLOTS = ADAPTERS * RANK
    T = GROUPS * FT
    assert SLOTS == P and 2 * POS == P

    x_pairs = x.rearrange("b c t -> (b c) t")
    out_pairs = out.rearrange("b c t -> (b c) t")
    bg_rows = bg.rearrange("n r f -> (n r) f")
    bu_rows = bu.rearrange("n r f -> (n r) f")
    bd_rows = bd.rearrange("n r f -> (n r) f")

    ds = bass.ds

    ctx = ExitStack()
    with ctx:
        def sb(name, shape, dt=f32, stack=ctx):
            return stack.enter_context(nc.sbuf_tensor(name, shape, dt))

        def sem(name):
            return ctx.enter_context(nc.semaphore(name))

        bank = [ctx.enter_context(nc.psum_tensor(f"bank{i}", [P, 512], f32)) for i in range(8)]

        X1 = sb("X1", [P, PAIRS, FEAT])
        ident = sb("ident", [P, P])
        mask2 = sb("mask2", [P, SAMPLES])
        w3raw = sb("w3raw", [P, PAIRS, POS])

        assert GROUPS == 4
        XT = sb("XT", [P, 2, KT, 2 * TOK], r32)
        DS, DQ = 4, GP // 2
        HALF = DS * RANK
        assert 2 * HALF == P
        AGU = sb("AGU", [P, 2, DQ, KT, P], r32)
        xh = [sb(f"xh{s}", [P, 2, FEAT], r32) for s in range(2)]
        early = ExitStack()
        ctx.enter_context(early)
        UT = sb("UT", [P, 2, 2 * TOK], r32, early)
        ad_raw = sb("ad_raw", [P, FT, SLOTS], f32, early)
        BDS = sb("BDS", [P, DQ, 2, FEAT], r32, early)

        GU = 2 * KT * P
        DMAS = 3
        NB = 2 * KT + 2 * DQ
        BSTEPS, RING = 2, 4
        CHUNKS = T // BSTEPS
        stage = [sb(f"stage{s}", [P, GU + FEAT], f32, early) for s in range(2)]
        adsel = sb("adsel", [P, RING, BSTEPS, DQ, HALF], f32, early)
        braw = sb("braw", [P, RING, 2 * DQ, BSTEPS * P], f32, early)
        gu = [sb(f"gu{s}", [P, 2, NB, P], r32, early) for s in range(2)]
        s_bload = sem("s_bload")
        s_wload = [sem(f"s_wload{s}") for s in range(2)]
        s_firsth, s_firstl = sem("s_firsth"), sem("s_firstl")
        s_guh, s_gul, s_up = sem("s_guh"), sem("s_gul"), sem("s_up")

        def later(n, least):
            return not isinstance(n, int) or n >= least

        def load_weights(eng, f, s):
            g2 = stage[s][:, 0:GU].rearrange("p (j k f) -> p j k f", j=2, k=KT)
            cols = ds(f * P, P)
            for j, w in enumerate((wg, wu)):
                eng.dma_start(g2[:, j, :, :], w.rearrange("(k p) f -> p k f", p=P)[:, :, cols]).then_inc(s_wload[s], 16)
            eng.dma_start(stage[s][:, GU:GU + FEAT], wd[cols, :]).then_inc(s_wload[s], 16)

        def parts(s, slot):
            return ((stage[s][:, 0:GU].rearrange("p (n f) -> p n f", f=P), slice(0, 2 * KT)),
                    (braw[:, ds(slot, 1), :, s * P:(s + 1) * P].rearrange("p a n f -> p (a n) f"), slice(2 * KT, NB)))

        def gu_high(act, t, s, n, slot):
            weights_high(act, t, s, n, slot)
            b_high(act, s, n, slot)

        def weights_high(act, t, s, n, slot):
            w, at = parts(s, slot)[0]
            act.wait_ge(s_wload[s], 16 * DMAS * (n + 1))
            if later(t, 2):
                act.wait_ge(s_up, t - 1)
            high = nc.scalar.activation(gu[s][:, 0, at, :], w, ACT.Copy)
            if isinstance(t, int) and t == 0:
                high.then_inc(s_firsth, 1)

        def b_high(act, s, n, slot):
            b, at = parts(s, slot)[1]
            act.wait_ge(s_bload, 16 * 2 * DQ * (n + 1))
            nc.scalar.activation(gu[s][:, 0, at, :], b, ACT.Copy).then_inc(s_guh, 1)

        def low(s, part):
            src, at = part
            return nc.vector.tensor_tensor(gu[s][:, 1, at, :], src, gu[s][:, 0, at, :].bitcast(f32), ALU.subtract)

        def gu_low(dve, t, s, slot):
            dve.wait_ge(s_guh, t + 1)
            w, b = parts(s, slot)
            low(s, w)
            low(s, b).then_inc(s_gul, 1)

        idx = sb("idx", [P, 3, SAMPLES], i32, early)
        us = sb("us", [P, 2, TOK], r32, early)
        idxf = sb("idxf", [P, 2, SAMPLES], f32, early)
        row_i = sb("row_i", [P, 4], i32, early)
        row_f = sb("row_f", [P, 4], f32, early)
        moves = sb("moves", [P, 5, HALF], r32, early)
        nothing = sb("nothing", [P, P], r32, early)
        own = sb("own", [P, DS], f32, early)
        pick = sb("pick", [P, PAIRS // 2, DS], f32, early)
        bsum = sb("bsum", [P, PAIRS // 2], f32, early)
        boffs = sb("boffs", [P, PAIRS // 2], i32, early)
        lane = sb("lane", [P, PAIRS], i32, early)
        offs = sb("offs", [P, 2, PAIRS], i32, early)
        scal = sb("scal", [P, ADAPTERS], f32, early)
        srow = sb("srow", [P, 1], f32, early)
        biasT = sb("biasT", [P, ADAPTERS], f32, early)
        napt = sb("napt", [P, ADAPTERS], i32, early)
        naptf = sb("naptf", [P, ADAPTERS], f32, early)
        beq = sb("beq", [P, PAIRS, ADAPTERS], f32, early)
        bias = sb("bias", [P, PAIRS], f32, early)
        raws = sb("raws", [P, KT * FEAT], f32, early)
        agu_raw = raws[:, 0:2 * KT * SLOTS].rearrange("p (j k n) -> p j k n", j=2, k=KT)
        w0raw = raws[:, 2 * KT * SLOTS:].rearrange("p (a d) -> p a d", d=POS)
        assert 2 * KT * SLOTS + PAIRS * POS == KT * FEAT and SLOTS * KT == FEAT
        w0bd = [sb(f"w0bd{s}", [P, 2, P], r32, early) for s in range(2)]
        x1s = [sb(f"x1s{s}", [P, FEAT], f32, early) for s in range(2)]
        hid = [sb(f"hid{s}", [P, TOK], f32, early) for s in range(2)]
        spare = [braw[:, RING - 1, 2 * s:2 * s + 2, :].rearrange("p n f -> p (n f)") for s in range(2)]
        assert 2 * BSTEPS * P == FEAT and GP == 4

        def x1_of(p, s):
            return x1s[s][:, :] if later(p, GP) or p < 2 else spare[s]

        assert DQ == 2 and KT * P == FEAT == TOK

        s_idx = [sem(f"s_idx{n}") for n in range(3)]
        s_small, s_tab, s_tab2, s_dch, s_pch = (sem(n) for n in
            ("s_small", "s_tab", "s_tab2", "s_dch", "s_pch"))
        s_ud = sem("s_ud")
        s_scal, s_w2 = sem("s_scal"), sem("s_w2")
        s_boffs, s_sel = sem("s_boffs"), sem("s_sel")
        s_adsel, s_asel, s_ah, s_al = sem("s_adsel"), sem("s_asel"), sem("s_ah"), sem("s_al")
        s_bdload, s_bdh, s_bdl, s_moves = sem("s_bdload"), sem("s_bdh"), sem("s_bdl"), sem("s_moves")
        s_consts, s_ident, s_offs = sem("s_consts"), sem("s_ident"), sem("s_offs")
        s_zero = sem("s_zero")
        s_xload = [sem(f"s_xload{p}") for p in range(GP)]
        s_xrest = sem("s_xrest")
        s_xkept = [sem(f"s_xkept{s}") for s in range(2)]
        s_w0first = [sem(f"s_w0first{p}") for p in range(GP)]
        s_w0 = [sem(f"s_w0_{s}") for s in range(2)]
        s_w3 = sem("s_w3")
        s_xh, s_w0h, s_xsplit, s_l0, s_x1 = sem("s_xh"), sem("s_w0h"), sem("s_xsplit"), sem("s_l0"), sem("s_x1")
        s_tr, s_xth, s_xtl, s_u, s_um, s_uh, s_ul = (sem(n) for n in
            ("s_tr", "s_xth", "s_xtl", "s_u", "s_um", "s_uh", "s_ul"))

        LORA = 1 + GP // 2
        DTOK = TOK // DQ
        assert FT == 4 * RING and LORA + 2 > RING and LORA < RING
        psL0, psT, psU, psA = bank[2:4], bank[4:6], bank[6:8], bank[7]

        wds = [sb(f"wds{s}", [P, 2, FEAT], r32, early) for s in range(2)]
        ads = [sb(f"ads{s}", [P, DQ, 2, HALF], r32, early) for s in range(2)]
        hs = [sb(f"hs{s}", [P, 2, TOK], r32, early) for s in range(2)]
        udc = sb("udc", [P, TOK], f32, early)
        uds = sb("uds", [P, 2, TOK], r32, early)

        psG, psUp, psD, psUd = bank[0], bank[1], bank[2:6], bank[6]

        s_wdh, s_wdl = sem("s_wdh"), sem("s_wdl")
        s_gate, s_silu, s_hid, s_hh, s_hl, s_down = (sem(n) for n in
            ("s_gate", "s_silu", "s_hid", "s_hh", "s_hl", "s_down"))
        s_tt, s_th, s_tl = sem("s_tt"), sem("s_th"), sem("s_tl")

        w2_raw = raws[:, :].rearrange("p (k f) -> p k f", k=KT)
        a2_raw = x1s[0]
        b2_raw = x1s[1][:, :].rearrange("p (k n) -> p k n", k=KT)
        W2T = XT[:, :, :, 0:FEAT]
        A2T = AGU[:, :, 0, :, :]
        B2T = AGU[:, :, 1, :, :].rearrange("p a k f -> p a (k f)")
        TABS = KT + 2
        tab = [(W2T[:, :, n, :], [w2_raw[:, k, n * P:(n + 1) * P] for k in range(KT)]) for n in range(KT)]
        tab.append((A2T.rearrange("p a k f -> p a (k f)"), [a2_raw[:, k * P:(k + 1) * P] for k in range(KT)]))
        tab.append((B2T, [b2_raw[:, k, :] for k in range(KT)]))
        tab_bank = [bank[7]] * KT + [bank[7], bank[0]]
        assert TOK == FEAT
        s_udm, s_udh, s_udl, s_lb, s_x2 = (sem(n) for n in ("s_udm", "s_udh", "s_udl", "s_lb", "s_x2"))

        x2s = [xh[s].bitcast(f32) for s in range(2)]
        c_x2 = [sem(f"c_x2_{s}") for s in range(2)]

        with nc.Block() as block:

            @block.sync
            def _(sp):
                def load_idx(n, v):
                    sp.dma_start(idx[:, n, :], v.partition_broadcast(P)).then_inc(s_idx[n], 16)

                def load_x(p):
                    sp.dma_start(X1[:, p, :], x_pairs[p * P:(p + 1) * P, :]).then_inc(s_xload[p], 16)

                def keep(p, s):
                    sp.wait_ge(s_x1, p + 1)
                    sp.dma_start(X1[:, ds(p, 1), :], x1_of(p, s)).then_inc(s_xkept[s], 16)

                def load(t, f, s):
                    sp.wait_ge(s_wdl, t - 1)
                    sp.wait_ge(s_gul, t - 1)
                    load_weights(sp, f, s)

                def inner(t0, p0=None):
                    if p0 is None:
                        with sp.Fori(1, FT // 2) as i:
                            for s in range(2):
                                load(t0 + 2 * i + s, 2 * i + s, s)
                        return
                    load(t0 + 2, 2, 0)
                    with sp.Fori(0, GP // 2) as i:
                        for s in range(2):
                            load(t0 + 3 + 2 * i + s, 3 + 2 * i + s, 1 - s)
                            keep(p0 + 2 * i + s, s)
                    load(t0 + GP + 3, GP + 3, 1)
                    with sp.Fori(GP // 2 + 2, FT // 2) as i:
                        for s in range(2):
                            load(t0 + 2 * i + s, 2 * i + s, s)

                def load_group(g):
                    sp.dma_start(X1[:, g * GP:(g + 1) * GP, :],
                                 x_pairs[g * TOK:(g + 1) * TOK, :].rearrange("(a p) t -> p a t", p=P)).then_inc(s_xrest, 16)

                load_idx(0, idx_a)
                load_x(0)
                load_x(1)
                load_idx(1, idx_b)
                load_x(2)
                load_idx(2, idx_c)
                load_x(3)
                for j, a in enumerate((ag, au)):
                    for k in range(KT):
                        sp.dma_start(agu_raw[:, j, k, :].rearrange("p (n r) -> p n r", n=ADAPTERS),
                                     a[:, k * P:(k + 1) * P, :].rearrange("n p r -> p n r")).then_inc(s_tab, 16)
                load_weights(sp, 0, 0)
                keep(0, 0)
                keep(1, 1)
                load_weights(sp, 1, 1)
                for n in range(ADAPTERS):
                    sp.dma_start(ad_raw[:, :, n * RANK:(n + 1) * RANK],
                                 ad[n].rearrange("(k p) r -> p k r", p=P)).then_inc(s_tab2, 16)
                keep(2, 0)
                keep(3, 1)
                load_group(1)
                inner(0, GP)
                for g in range(2, GROUPS):
                    load_group(g)
                with sp.Fori(1, GROUPS - 1) as g:
                    for s in range(2):
                        load(FT * g + s, s, s)
                    inner(FT * g, GP * g + GP)
                for s in range(2):
                    load(FT * (GROUPS - 1) + s, s, s)
                inner(FT * (GROUPS - 1))
                for s in range(2):
                    sp.wait_ge(s_xkept[s], 16 * PAIRS // 2)
                sp.wait_ge(s_x2, 1)
                sp.wait_ge(s_l0, PAIRS)
                for s in range(2):
                    sp.dma_start(x2s[s][:, :, :], X1[:, 2 * s:2 * s + 2, :]).then_inc(c_x2[s], 16)

            @block.gpsimd
            def _(pool):
                nc.gpsimd.iota(row_i[:, 0:1], [[0, 1]], base=0, channel_multiplier=1).then_inc(s_consts, 1)
                nc.gpsimd.iota(lane[:, :], [[0, PAIRS]], base=0, channel_multiplier=1).then_inc(s_consts, 1)
                nc.gpsimd.iota(napt[:, :], [[1, ADAPTERS]], base=0, channel_multiplier=0).then_inc(s_consts, 1)
                nc.gpsimd.memset(ident[:, :], 0.0).then_inc(s_pch, 1)
                pool.wait_ge(s_pch, 1)
                nc.gpsimd.affine_select(out=ident[:, :], in_=ident[:, :], compare_op=ALU.not_equal, fill=1.0, base=0,
                                        pattern=[[-1, P]], channel_multiplier=1).then_inc(s_ident, 1)
                pool.wait_ge(s_offs, 1)
                rows0 = w0.rearrange("n c d -> (n c) d")
                rows3 = w3.rearrange("n c d -> (n c) d")

                def gather_w0(p):
                    s = p % 2
                    if p >= GP + 2:
                        pool.wait_ge(s_w0[s], 16 * (p // 2 - GP // 2))
                    nc.gpsimd.indirect_dma_start(
                        w0raw[:, p, :], None, rows0,
                        bass.IndirectOffsetOnAxis(offs[:, 0, p:p + 1].bitcast(u32), 0)).then_inc(
                            s_w0first[p] if p < GP else s_w0[s], 16)

                def gather_b(c):
                    if c >= RING:
                        pool.wait_ge(s_gul, BSTEPS * (c - RING + 1))
                    if c >= 1:
                        pool.wait_ge(s_bload, 16 * 2 * DQ * c)
                    if c == RING - 1:
                        pool.wait_ge(s_tr, GP)
                        for s in range(2):
                            pool.wait_ge(s_xkept[s], 16 * GP // 2)
                    g, f = c * BSTEPS // FT, c * BSTEPS % FT
                    for j, rows in enumerate((bg_rows, bu_rows)):
                        for q in range(DQ):
                            nc.gpsimd.indirect_dma_start(
                                braw[:, c % RING, DQ * j + q, :], None, rows,
                                bass.IndirectOffsetOnAxis(boffs[:, DQ * g + q:DQ * g + q + 1].bitcast(u32), 0),
                                element_offset=f * P).then_inc(s_bload, 16)

                def adapters(g):
                    return [nc.gpsimd.value_load(idx[0:1, 0, n:n + 1], min_val=0, max_val=ADAPTERS - 1) * RANK
                            for n in range(2 * GP * g, 2 * GP * (g + 1))]

                def select_ad(c, cols):
                    if c >= RING:
                        pool.wait_ge(s_wdl, BSTEPS * (c - RING + 1))
                    f = c * BSTEPS % FT
                    for n, col in enumerate(cols):
                        last = nc.gpsimd.tensor_copy(
                            adsel[:, c % RING, :, n // DS, n % DS * RANK:(n % DS + 1) * RANK],
                            ad_raw[:, f:f + BSTEPS, ds(col, RANK)])
                    last.then_inc(s_adsel, 1)

                def select_a(g, cols):
                    if g >= 1:
                        pool.wait_ge(s_tr, GP * (g + 1))
                        for s in range(2):
                            pool.wait_ge(s_xkept[s], 16 * GP * (g + 1) // 2)
                    for n, col in enumerate(cols):
                        raw = (x1s if g >= 1 else hid)[n // DS][:, :].rearrange("p (k j m) -> p j k m", k=KT, j=2)
                        at = n % DS * RANK
                        last = nc.gpsimd.tensor_copy(raw[:, :, :, at:at + RANK], agu_raw[:, :, :, ds(col, RANK)])
                    last.then_inc(s_asel, 1)

                def gather_bd(g):
                    pool.wait_ge(s_al, min(g + 2, GROUPS))
                    if g >= 1:
                        pool.wait_ge(s_bdl, g)
                    for q in range(DQ):
                        nc.gpsimd.indirect_dma_start(
                            x1s[q][:, :], None, bd_rows,
                            bass.IndirectOffsetOnAxis(boffs[:, DQ * g + q:DQ * g + q + 1].bitcast(u32), 0)).then_inc(s_bdload, 16)

                for p in range(GP):
                    gather_w0(p)
                pool.wait_ge(s_boffs, 1)
                gather_b(0)
                pool.wait_ge(s_idx[0], 16)
                cols = adapters(0)
                pool.wait_ge(s_tab, 16 * 2 * KT)
                select_a(0, cols)
                for p in range(GP, GP + 2):
                    gather_w0(p)
                pool.wait_ge(s_tab2, 16 * ADAPTERS)
                for c in range(RING):
                    if c >= 1:
                        gather_b(c)
                    select_ad(c, cols)
                for p in range(GP + 2, PAIRS):
                    gather_w0(p)
                pool.wait_ge(s_offs, 2)
                per_group = FT // BSTEPS
                for c in range(RING, CHUNKS):
                    g = c // per_group
                    if c % per_group == per_group - 2 and g + 1 < GROUPS:
                        next_cols = adapters(g + 1)
                    if c % per_group == per_group - 1 and g + 1 < GROUPS:
                        select_a(g + 1, next_cols)
                    if c % per_group == 0:
                        cols = next_cols
                    if c % per_group == 2 and g >= 1:
                        gather_bd(g - 1)
                    if c == CHUNKS - RING + 2:
                        gather_bd(g)
                    gather_b(c)
                    select_ad(c, cols)
                    if g >= 1 and c - per_group < PAIRS:
                        p = c - per_group
                        nc.gpsimd.indirect_dma_start(
                            w3raw[:, p, :], None, rows3,
                            bass.IndirectOffsetOnAxis(offs[:, 1, p:p + 1].bitcast(u32), 0)).then_inc(s_w3, 16)
                assert CHUNKS - per_group >= PAIRS
                pool.wait_ge(s_bdload, 16 * DQ * GROUPS)
                pool.wait_ge(s_w3, 16 * PAIRS)

            @block.scalar
            def _(act):
                with nc.allow_non_contiguous_dma(reason="512 values, once"):
                    for s in range(2):
                        act.dma_start(biasT[s * POS:(s + 1) * POS, :], bias0.rearrange("n d -> d n")).then_inc(s_small, 16)
                act.dma_start(scal[:, :], scal2.partition_broadcast(P)).then_inc(s_scal, 16)

                def x_high(p, s):
                    if not later(p, GP):
                        act.wait_ge(s_xload[p], 16)
                    if later(p, 2):
                        act.wait_ge(s_l0, p - 1)
                    nc.scalar.activation(xh[s][:, 0, :], X1[:, ds(p, 1), :].rearrange("p a t -> p (a t)"), ACT.Copy).then_inc(s_xh, 1)

                def w0_high(p, s, n):
                    if later(p, GP):
                        act.wait_ge(s_w0[s], 16 * (n + 1 - GP // 2))
                    else:
                        act.wait_ge(s_w0first[p], 16)
                    for h in range(2):
                        last = nc.scalar.activation(w0bd[s][h * POS:(h + 1) * POS, 0, h * POS:(h + 1) * POS],
                                                    w0raw[h * POS:(h + 1) * POS, ds(p, 1), :], ACT.Copy)
                    last.then_inc(s_w0h, 1)

                def xt_high(p, col, bank):
                    act.wait_ge(s_tr, p + 1)
                    nc.scalar.activation(XT[:, 0, :, ds(col, P)],
                                         bank[:, :].rearrange("p (k t) -> p k t", k=KT), ACT.Copy).then_inc(s_xth, 1)

                def a_high(g):
                    act.wait_ge(s_asel, g + 1)
                    if later(g, 1):
                        act.wait_ge(s_u, g)
                    for q in range(DQ):
                        last = nc.scalar.activation(AGU[:, 0, q, :, :].rearrange("p k m -> p (k m)"),
                                                    (x1s if later(g, 1) else hid)[q][:, :], ACT.Copy)
                    last.then_inc(s_ah, 1)

                def bd_high(g):
                    act.wait_ge(s_bdload, 16 * DQ * (g + 1))
                    if later(g, 1):
                        act.wait_ge(s_lb, g)
                    for q in range(DQ):
                        last = nc.scalar.activation(BDS[:, q, 0, :], x1s[q][:, :], ACT.Copy)
                    last.then_inc(s_bdh, 1)

                def u_high(g):
                    act.wait_ge(s_u, g + 1)
                    nc.scalar.activation(us[:, 0, :], psA[:, :], ACT.Copy).then_inc(s_uh, 1)

                def wd_high(t, s, n, slot):
                    act.wait_ge(s_adsel, n + 1)
                    if later(t, 2):
                        act.wait_ge(s_down, t - 1)
                    nc.scalar.activation(ads[s][:, :, 0, :], adsel[:, ds(slot, 1), s, :, :].rearrange("p a q m -> p (a q) m"),
                                         ACT.Copy)
                    nc.scalar.activation(wds[s][:, 0, :], stage[s][:, GU:GU + FEAT], ACT.Copy).then_inc(s_wdh, 1)

                def silu(t, s):
                    act.wait_ge(s_gate, t + 1)
                    if later(t, 2):
                        act.wait_ge(s_hl, t - 1)
                    nc.scalar.activation(hid[s][:, :], psG[:, :], ACT.Silu).then_inc(s_silu, 1)

                def hid_high(t, s):
                    act.wait_ge(s_hid, t + 1)
                    if later(t, 2):
                        act.wait_ge(s_down, t - 1)
                    nc.scalar.activation(hs[s][:, 0, :], hid[s][:, :], ACT.Copy).then_inc(s_hh, 1)

                def rest(t, s, n, before):
                    wd_high(t - 1, 1 - s, n + s - 1, before)
                    silu(t - 1, 1 - s)

                def step(t, s, n, slot, before):
                    gu_high(act, t, s, n, slot)
                    rest(t, s, n, before)

                def ud_high(g):
                    act.wait_ge(s_udm, g + 1)
                    if later(g, 1):
                        act.wait_ge(s_lb, g)
                    nc.scalar.activation(uds[:, 0, :], udc[:, :], ACT.Copy).then_inc(s_udh, 1)

                def table_high(n):
                    act.wait_ge(s_tt, n + 1)
                    nc.scalar.activation(tab[n][0][:, 0, :], tab_bank[n][:, :], ACT.Copy).then_inc(s_th, 1)

                def inner(t0, n0, g=None, cn=None):
                    def plain(i, s, slot, before):
                        step(t0 + 2 * i + s, s, n0 + i, slot, before)
                        hid_high(t0 + 2 * i + s - 1, 1 - s)

                    if g is None:
                        with act.Fori(1, RING) as i:
                            for s in range(2):
                                plain(i, s, i, i + s - 1)
                        bd_high(GROUPS - 1)
                        for s in range(2):
                            plain(RING, s, 0, 0 if s else RING - 1)
                            for n in range(s * KT // 2, (s + 1) * KT // 2):
                                table_high(n)
                        act.wait_ge(s_bdl, GROUPS)
                        act.dma_start(a2_raw[:, :], a2.rearrange("n r f -> (n r) f")).then_inc(s_tab, 16)
                        for k in range(KT):
                            act.dma_start(b2_raw[:, k, :].rearrange("p (n r) -> p n r", n=ADAPTERS),
                                          b2[:, k * P:(k + 1) * P, :].rearrange("n p r -> p n r")).then_inc(s_tab, 16)
                        with act.Fori(RING + 1, 2 * RING) as i:
                            for s in range(2):
                                plain(i, s, i - RING, i - RING + s - 1)
                        return
                    with act.Fori(1, LORA) as i:
                        for s in range(2):
                            p = GP * g + 2 * i + s - 2
                            x_high(p, s)
                            w0_high(p, s, GP // 2 * g + i - 1)
                            plain(i, s, i, i + s - 1)
                            xt_high(p, cn + (2 * i + s - 2) * P, psA)
                    for j in range(2):
                        for s in range(2):
                            plain(LORA + j, s, (LORA + j) % RING, (LORA + j + s - 1) % RING)
                            if (j, s) == (0, 0):
                                a_high(g)
                            if (j, s) == (0, 1):
                                u_high(g)
                    with act.Fori(LORA + 2, 2 * RING) as i:
                        for s in range(2):
                            plain(i, s, i - RING, i - RING + s - 1)

                act.wait_ge(s_zero, 2)
                for p in range(2):
                    x_high(p, p)
                for p in range(2):
                    w0_high(p, p, 0)
                x_high(2, 0)
                w0_high(2, 0, 1)
                x_high(3, 1)
                w0_high(3, 1, 1)
                xt_high(0, 0, psT[0])
                xt_high(1, P, psT[1])
                for p in range(2, GP):
                    xt_high(p, p * P, psT[p % 2])
                weights_high(act, 0, 0, 0, 0)
                a_high(0)
                b_high(act, 0, 0, 0)
                gu_high(act, 1, 1, 0, 0)
                u_high(0)
                wd_high(0, 0, 0, 0)
                silu(0, 0)
                hid_high(0, 0)
                act.wait_ge(s_xrest, 16)
                inner(0, 0, 1, TOK)
                act.wait_ge(s_xrest, 16 * (GROUPS - 1))
                def turn(g):
                    t0, n0 = FT * g, FT // 2 * g
                    step(t0, 0, n0, 0, RING - 1)
                    hid_high(t0 - 1, 1)
                    gu_high(act, t0 + 1, 1, n0, 0)
                    bd_high(g - 1)
                    ud_high(g - 1)
                    rest(t0 + 1, 1, n0, 0)
                    hid_high(t0, 0)

                with act.Fori(1, GROUPS - 1) as g:
                    turn(g)
                    inner(FT * g, FT // 2 * g, g + 1, (g - 1) * TOK)
                act.wait_ge(s_xsplit, PAIRS)
                act.wait_ge(s_asel, GROUPS)
                act.dma_start(w2_raw, w2.rearrange("(k p) f -> p k f", p=P)).then_inc(s_w2, 16)
                turn(GROUPS - 1)
                inner(FT * (GROUPS - 1), FT // 2 * (GROUPS - 1))
                wd_high(T - 1, 1, T // 2 - 1, RING - 1)
                silu(T - 1, 1)
                hid_high(T - 1, 1)

                ud_high(GROUPS - 1)
                for n in range(KT, TABS):
                    table_high(n)

            @block.vector
            def _(dve):
                chain = [0]

                def link(ins):
                    chain[0] += 1
                    ins.then_inc(s_dch, 1)
                    dve.wait_ge(s_dch, chain[0])

                for s in range(2):
                    nc.vector.memset(w0bd[s][:, :, :].bitcast(f32), 0.0).then_inc(s_zero, 1)
                dve.wait_ge(s_consts, 3)
                link(nc.vector.tensor_scalar(lane[:, :], lane[:, :], POS - 1, None, ALU.bitwise_and))
                def offsets(j, n):
                    dve.wait_ge(s_idx[n], 16)
                    for h in range(2):
                        rows = slice(h * POS, (h + 1) * POS)
                        shifted = nc.vector.tensor_scalar(
                            offs[rows, j, :], idx[rows, n, :].rearrange("p (q h) -> p q h", h=2)[:, :, h],
                            POS.bit_length() - 1, None, ALU.logical_shift_left)
                    link(shifted)
                    nc.vector.tensor_tensor(offs[:, j, :], offs[:, j, :], lane[:, :], ALU.add).then_inc(s_offs, 1)

                def rows_of_ranks():
                    link(nc.vector.tensor_scalar(row_i[:, 1:2], row_i[:, 0:1], RANK.bit_length() - 1, None, ALU.logical_shift_right))
                    nc.vector.tensor_scalar(row_i[:, 2:3], row_i[:, 0:1], RANK - 1, None, ALU.bitwise_and)
                    link(nc.vector.tensor_scalar(row_i[:, 3:4], row_i[:, 1:2], DS - 1, None, ALU.bitwise_and))
                    nc.vector.tensor_copy(row_f[:, :], row_i[:, :])
                    link(nc.vector.tensor_copy(naptf[:, :], napt[:, :]))
                    link(nc.vector.tensor_scalar(own[:, :], naptf[:, 0:DS], row_f[:, 3:4], None, ALU.is_equal))

                def gather_rows():
                    link(nc.vector.tensor_copy(idxf[:, 0, :], idx[:, 0, :]))
                    link(nc.vector.tensor_tensor(pick[:, :, :], idxf[:, 0, :].rearrange("p (d n) -> p d n", n=DS),
                                                 own[:, :].unsqueeze(1).to_broadcast([P, PAIRS // 2, DS]), ALU.mult))
                    link(nc.vector.tensor_reduce(bsum[:, :], pick[:, :, :], X, ALU.add))
                    link(nc.vector.tensor_scalar(bsum[:, :], bsum[:, :], float(RANK), row_f[:, 2:3], ALU.mult, ALU.add))
                    nc.vector.tensor_copy(boffs[:, :], bsum[:, :]).then_inc(s_boffs, 1)

                def move_table():
                    nc.vector.memset(nothing[:, :].bitcast(f32), 0.0)
                    link(nc.vector.memset(moves[:, :, :].bitcast(f32), 0.0))
                    dve.wait_ge(s_ident, 1)
                    for j in range(2):
                        last = nc.vector.tensor_copy(moves[:, 2 * j + 1, :], ident[:, j * HALF:(j + 1) * HALF])
                    last.then_inc(s_moves, 1)

                def biases():
                    dve.wait_ge(s_small, 16 * 2)
                    for h in range(2):
                        rows = slice(h * POS, (h + 1) * POS)
                        sel = idxf[rows, 0, :].rearrange("p (q h) -> p q h", h=2)[:, :, h:h + 1]
                        link(nc.vector.tensor_tensor(beq[rows, :, :], sel.to_broadcast([POS, PAIRS, ADAPTERS]),
                                                     naptf[rows, :].unsqueeze(1).to_broadcast([POS, PAIRS, ADAPTERS]),
                                                     ALU.is_equal))
                    link(nc.vector.tensor_tensor(beq[:, :, :], beq[:, :, :],
                                                 biasT[:, :].unsqueeze(1).to_broadcast([P, PAIRS, ADAPTERS]), ALU.mult))
                    link(nc.vector.tensor_reduce(bias[:, :], beq[:, :, :], X, ALU.add))

                def masks():
                    dve.wait_ge(s_idx[1], 16)
                    dve.wait_ge(s_scal, 16)
                    link(nc.vector.tensor_copy(idxf[:, 1, :], idx[:, 1, :]))
                    link(nc.vector.tensor_scalar(naptf[:, :], naptf[:, :], row_f[:, 1:2], None, ALU.is_equal))
                    link(nc.vector.tensor_tensor(naptf[:, :], naptf[:, :], scal[:, :], ALU.mult))
                    link(nc.vector.tensor_reduce(srow[:, :], naptf[:, :], X, ALU.add))
                    link(nc.vector.tensor_scalar(mask2[:, :], idxf[:, 1, :], row_f[:, 1:2], srow[:, 0:1],
                                                 ALU.is_equal, ALU.mult))

                def x_low(p, s):
                    dve.wait_ge(s_xh, p + 1)
                    nc.vector.tensor_tensor(xh[s][:, 1, :], X1[:, ds(p, 1), :].rearrange("p a t -> p (a t)"), xh[s][:, 0, :].bitcast(f32), ALU.subtract)
                    dve.wait_ge(s_w0h, p + 1)
                    for h in range(2):
                        rows = slice(h * POS, (h + 1) * POS)
                        last = nc.vector.tensor_tensor(w0bd[s][rows, 1, rows], w0raw[rows, ds(p, 1), :].rearrange("p a d -> p (a d)"),
                                                       w0bd[s][rows, 0, rows].bitcast(f32), ALU.subtract)
                    last.then_inc(s_xsplit, 1)

                def x1(p, s, n, bank):
                    dve.wait_ge(s_l0, p + 1)
                    if later(p, GP):
                        dve.wait_ge(s_tr, p - 1)
                        dve.wait_ge(s_xkept[s], 16 * n)
                    nc.vector.scalar_tensor_tensor(out=x1_of(p, s), in0=bank[:, :], scalar=bias[:, ds(p, 1)],
                                                   in1=X1[:, ds(p, 1), :].rearrange("p a t -> p (a t)"),
                                                   op0=ALU.add, op1=ALU.add).then_inc(s_x1, 1)

                def xt_low(p, col, bank):
                    dve.wait_ge(s_xth, p + 1)
                    nc.vector.tensor_tensor(XT[:, 1, :, ds(col, P)],
                                            bank[:, :].rearrange("p (k t) -> p k t", k=KT),
                                            XT[:, 0, :, ds(col, P)].bitcast(f32), ALU.subtract).then_inc(s_xtl, 1)

                def a_low(g):
                    dve.wait_ge(s_ah, g + 1)
                    for q in range(DQ):
                        last = nc.vector.tensor_tensor(AGU[:, 1, q, :, :].rearrange("p k m -> p (k m)"),
                                                       (x1s if later(g, 1) else hid)[q][:, :],
                                                       AGU[:, 0, q, :, :].rearrange("p k m -> p (k m)").bitcast(f32),
                                                       ALU.subtract)
                    last.then_inc(s_al, 1)

                def bd_low(g):
                    dve.wait_ge(s_bdh, g + 1)
                    for q in range(DQ):
                        last = nc.vector.tensor_tensor(BDS[:, q, 1, :], x1s[q][:, :], BDS[:, q, 0, :].bitcast(f32),
                                                       ALU.subtract)
                    last.then_inc(s_bdl, 1)

                def u_low(g):
                    dve.wait_ge(s_uh, g + 1)
                    nc.vector.tensor_tensor(us[:, 1, :], psA[:, :], us[:, 0, :].bitcast(f32),
                                            ALU.subtract).then_inc(s_ul, 1)

                def u_own(g, j, c, bank):
                    dve.wait_ge(s_sel, 2 * g + j + 1)
                    nc.vector.tensor_tensor(UT[:, j, ds(c, TOK)].rearrange("p (q n t) -> p q n t", q=DQ, n=DS),
                                            bank[:, :].rearrange("p (q n t) -> p q n t", q=DQ, n=DS),
                                            own[:, :].unsqueeze(1).unsqueeze(3).to_broadcast([P, DQ, DS, POS]),
                                            ALU.mult).then_inc(s_um, 1)

                def wd_low(t, s, slot):
                    dve.wait_ge(s_wdh, t + 1)
                    nc.vector.tensor_tensor(ads[s][:, :, 1, :], adsel[:, ds(slot, 1), s, :, :].rearrange("p a q m -> p (a q) m"),
                                            ads[s][:, :, 0, :].bitcast(f32), ALU.subtract)
                    nc.vector.tensor_tensor(wds[s][:, 1, :], stage[s][:, GU:GU + FEAT], wds[s][:, 0, :].bitcast(f32),
                                            ALU.subtract).then_inc(s_wdl, 1)

                def gated(t, s):
                    dve.wait_ge(s_up, t + 1)
                    dve.wait_ge(s_silu, t + 1)
                    nc.vector.tensor_tensor(hid[s][:, :], psUp[:, :], hid[s][:, :], ALU.mult).then_inc(s_hid, 1)

                def hid_low(t, s):
                    dve.wait_ge(s_hh, t + 1)
                    nc.vector.tensor_tensor(hs[s][:, 1, :], hid[s][:, :], hs[s][:, 0, :].bitcast(f32),
                                            ALU.subtract).then_inc(s_hl, 1)

                def ud_mask(g):
                    dve.wait_ge(s_ud, g + 1)
                    nc.vector.tensor_tensor(udc[:, :].rearrange("p (q n t) -> p q n t", q=DQ, n=DS),
                                            psUd[:, :].rearrange("p (q n t) -> p q n t", q=DQ, n=DS),
                                            own[:, :].unsqueeze(1).unsqueeze(3).to_broadcast([P, DQ, DS, POS]),
                                            ALU.mult).then_inc(s_udm, 1)
                    dve.wait_ge(s_udh, g + 1)
                    nc.vector.tensor_tensor(uds[:, 1, :], udc[:, :], uds[:, 0, :].bitcast(f32),
                                            ALU.subtract).then_inc(s_udl, 1)

                def x2(g):
                    dve.wait_ge(s_lb, g + 1)
                    for j in range(GP):
                        dst = X1[:, ds(GP * g + j, 1), :].rearrange("p a f -> p (a f)")
                        last = nc.vector.tensor_tensor(dst, psD[j][:, :], dst, ALU.add)
                    last.then_inc(s_x2, 1)

                def rest(t, s, before):
                    wd_low(t - 1, 1 - s, before)
                    gated(t - 1, 1 - s)
                    hid_low(t - 1, 1 - s)

                def step(t, s, slot, before):
                    gu_low(dve, t, s, slot)
                    rest(t, s, before)

                def table_low(n):
                    dve.wait_ge(s_th, n + 1)
                    nc.vector.tensor_tensor(tab[n][0][:, 1, :], tab_bank[n][:, :], tab[n][0][:, 0, :].bitcast(f32),
                                            ALU.subtract).then_inc(s_tl, 1)

                def inner(t0, g=None, cn=None):
                    def plain(i, s, slot, before):
                        step(t0 + 2 * i + s, s, slot, before)

                    if g is None:
                        with dve.Fori(1, RING) as i:
                            for s in range(2):
                                plain(i, s, i, i + s - 1)
                        bd_low(GROUPS - 1)
                        for s in range(2):
                            plain(RING, s, 0, 0 if s else RING - 1)
                            for n in range(s * KT // 2, (s + 1) * KT // 2):
                                table_low(n)
                        with dve.Fori(RING + 1, 2 * RING) as i:
                            for s in range(2):
                                plain(i, s, i - RING, i - RING + s - 1)
                        return
                    with dve.Fori(1, LORA) as i:
                        for s in range(2):
                            p = GP * g + 2 * i + s - 2
                            x_low(p, s)
                            plain(i, s, i, i + s - 1)
                            x1(p, s, GP // 2 * g + i - 1, psA)
                            xt_low(p, cn + (2 * i + s - 2) * P, psA)
                    for j in range(2):
                        for s in range(2):
                            plain(LORA + j, s, (LORA + j) % RING, (LORA + j + s - 1) % RING)
                            if (j, s) == (0, 0):
                                a_low(g)
                            if (j, s) == (0, 1):
                                u_low(g)
                            if j == 1:
                                u_own(g, s, cn, psA)
                    with dve.Fori(LORA + 2, 2 * RING) as i:
                        for s in range(2):
                            plain(i, s, i - RING, i - RING + s - 1)

                def turn(g):
                    step(FT * g, 0, 0, RING - 1)
                    gu_low(dve, FT * g + 1, 1, 0)
                    bd_low(g - 1)
                    ud_mask(g - 1)
                    rest(FT * g + 1, 1, 0)
                    x2(g - 1)

                rows_of_ranks()
                offsets(0, 0)
                gather_rows()
                biases()
                x_low(0, 0)
                x_low(1, 1)
                x1(0, 0, 0, psL0[0])
                x_low(2, 0)
                x1(1, 1, 0, psL0[1])
                x_low(3, 1)
                xt_low(0, 0, psT[0])
                x1(2, 0, 1, psL0[0])
                xt_low(1, P, psT[1])
                x1(3, 1, 1, psL0[1])
                for p in range(2, GP):
                    xt_low(p, p * P, psT[p % 2])
                dve.wait_ge(s_firsth, 1)
                w, b = parts(0, 0)
                low(0, w).then_inc(s_firstl, 1)
                move_table()
                a_low(0)
                dve.wait_ge(s_guh, 1)
                low(0, b).then_inc(s_gul, 1)
                gu_low(dve, 1, 1, 0)
                u_low(0)
                u_own(0, 0, 0, psU[1])
                u_own(0, 1, 0, psU[0])
                wd_low(0, 0, 0)
                gated(0, 0)
                hid_low(0, 0)
                offsets(1, 2)
                masks()
                inner(0, 1, TOK)
                with dve.Fori(1, GROUPS - 1) as g:
                    turn(g)
                    inner(FT * g, g + 1, (g - 1) * TOK)
                turn(GROUPS - 1)
                inner(FT * (GROUPS - 1))
                wd_low(T - 1, 1, RING - 1)
                gated(T - 1, 1)
                hid_low(T - 1, 1)

                ud_mask(GROUPS - 1)
                for n in range(KT, TABS):
                    table_low(n)

            @block.tensor
            def _(pe):
                def layer0(p, s, bank):
                    pe.wait_ge(s_xsplit, p + 1)
                    if bank is psA:
                        pe.wait_ge(s_xtl, p)
                    elif p >= 2:
                        pe.wait_ge(s_x1, p - 1)
                    for n, (a, b) in enumerate(((0, 0), (0, 1), (1, 0))):
                        last = nc.tensor.matmul(bank[:, :], w0bd[s][:, a, :], xh[s][:, b, :], start=(n == 0), stop=(n == 2))
                    last.then_inc(s_l0, 1)

                def transposes(p, s, bank):
                    pe.wait_ge(s_x1, p + 1)
                    if bank is not psA and p >= 2:
                        pe.wait_ge(s_xtl, p - 1)
                    for k in range(KT):
                        last = nc.tensor.transpose(bank[:, k * P:(k + 1) * P], x1_of(p, s)[:, k * P:(k + 1) * P], ident[:, :])
                    last.then_inc(s_tr, 1)

                def lora_in(g, c):
                    pe.wait_ge(s_xtl, GP * g + GP)
                    pe.wait_ge(s_al, g + 1)
                    for q in range(DQ):
                        for k in range(KT):
                            for n, (a, b) in enumerate(((0, 0), (0, 1), (1, 0))):
                                last = nc.tensor.matmul(psA[:, q * DTOK:(q + 1) * DTOK], AGU[:, a, q, k, :],
                                                        XT[:, b, k, ds(c + q * DTOK, DTOK)],
                                                        start=(k == 0 and n == 0), stop=(k == KT - 1 and n == 2))
                    last.then_inc(s_u, 1)

                def select(g, j, bank):
                    pe.wait_ge(s_ul, g + 1)
                    if later(g, 1) and j == 1:
                        pe.wait_ge(s_um, 2 * g + 1)
                    for a in range(2):
                        at = 2 * j + 1 - a
                        last = nc.tensor.matmul(bank[:, :], moves[:, at:at + 2, :].rearrange("p a m -> p (a m)"),
                                                us[:, a, :], start=(a == 0), stop=(a == 1))
                    last.then_inc(s_sel, 1)

                def half(j, s, c, psum, done, ks=range(KT + 1)):
                    for k in ks:
                        if k < KT:
                            for n, (a, b) in enumerate(((0, 0), (0, 1), (1, 0))):
                                nc.tensor.matmul(psum[:, :], gu[s][:, a, KT * j + k, :], XT[:, b, k, ds(c, TOK)],
                                                 start=(k == 0 and n == 0), stop=False)
                            continue
                        for q in range(DQ):
                            for a in range(2):
                                last = nc.tensor.matmul(psum[:, q * DTOK:(q + 1) * DTOK],
                                                        gu[s][:, a, 2 * KT + DQ * j + q, :],
                                                        UT[:, j, ds(c + q * DTOK, DTOK)],
                                                        start=False, stop=(q == DQ - 1 and a == 1))
                        last.then_inc(done, 1)

                def gate(t, s, c):
                    pe.wait_ge(s_gul, t + 1)
                    if later(t, 1):
                        pe.wait_ge(s_silu, t)
                    half(0, s, c, psG, s_gate)

                def up(t, s, c):
                    if later(t, 1):
                        pe.wait_ge(s_hid, t)
                    half(1, s, c, psUp, s_up)

                def down(t, s, first=False, final=False):
                    pe.wait_ge(s_hl, t + 1)
                    pe.wait_ge(s_wdl, t + 1)

                    def ranks():
                        if first:
                            nc.tensor.matmul(psUd[:, :], nothing[:, :], hs[s][:, 0, :], start=True, stop=False)
                        for q in range(DQ):
                            for b in range(2):
                                last = nc.tensor.matmul(psUd[:, q * DTOK:(q + 1) * DTOK],
                                                        ads[s][:, q, :, :].rearrange("p a m -> p (a m)"),
                                                        hs[s][:, b, q * DTOK:(q + 1) * DTOK],
                                                        start=False, stop=(final and q == DQ - 1 and b == 1))
                        return last

                    if final:
                        ranks().then_inc(s_ud, 1)
                    for j in range(GP):
                        for n, (a, b) in enumerate(((0, 0), (0, 1), (1, 0))):
                            last = nc.tensor.matmul(psD[j][:, :], hs[s][:, a, j * P:(j + 1) * P], wds[s][:, b, :],
                                                    start=(first and n == 0), stop=False)
                    if not final:
                        last = ranks()
                    last.then_inc(s_down, 1)

                def lora_down(g):
                    pe.wait_ge(s_udl, g + 1)
                    pe.wait_ge(s_bdl, g + 1)
                    for j in range(GP):
                        for n, (a, b) in enumerate(((0, 0), (0, 1), (1, 0))):
                            last = nc.tensor.matmul(psD[j][:, :], uds[:, a, j * P:(j + 1) * P], BDS[:, j * DQ // GP, b, :],
                                                    start=False, stop=(n == 2))
                    last.then_inc(s_lb, 1)

                def table(n):
                    if 1 <= n < KT:
                        pe.wait_ge(s_tl, n)
                    for k in range(KT):
                        last = nc.tensor.transpose(tab_bank[n][:, k * P:(k + 1) * P], tab[n][1][k], ident[:, :])
                    last.then_inc(s_tt, 1)

                def inner(t0, c, g=None, cn=None):
                    def plain(i):
                        for s in range(2):
                            t = t0 + 2 * i + s
                            gate(t, s, c)
                            up(t, s, c)
                            down(t - 1, 1 - s)

                    if g is not None:
                        with pe.Fori(1, 1 + GP // 2) as i:
                            for s in range(2):
                                t, p = t0 + 2 * i + s, GP * g + 2 * i + s - 2
                                layer0(p, s, psA)
                                gate(t, s, c)
                                transposes(p, s, psA)
                                up(t, s, c)
                                down(t - 1, 1 - s)
                        for j in range(2):
                            for s in range(2):
                                t = t0 + 2 * (LORA + j) + s
                                if (j, s) == (0, 1):
                                    lora_in(g, cn)
                                if j == 1:
                                    select(g, s, psA)
                                gate(t, s, c)
                                up(t, s, c)
                                down(t - 1, 1 - s)
                    else:
                        with pe.Fori(1, RING) as i:
                            plain(i)
                        pe.wait_ge(s_w2, 16)
                        for s in range(2):
                            t = t0 + 2 * RING + s
                            table(2 * s)
                            gate(t, s, c)
                            table(2 * s + 1)
                            up(t, s, c)
                            down(t - 1, 1 - s)
                        assert KT == 4
                    with pe.Fori(RING + 1 if g is None else LORA + 2, FT // 2) as i:
                        plain(i)

                def turn(g, c):
                    t0 = FT * g
                    pe.wait_ge(s_um, 2 * g + 2)
                    gate(t0, 0, c)
                    down(t0 - 1, 1, final=True)
                    up(t0, 0, c)
                    gate(t0 + 1, 1, c)
                    lora_down(g - 1)
                    up(t0 + 1, 1, c)
                    pe.wait_ge(s_x2, g)
                    down(t0, 0, first=True)

                layer0(0, 0, psL0[0])
                pe.wait_ge(s_ident, 1)
                for p in range(1, GP):
                    layer0(p, p % 2, psL0[p % 2])
                    transposes(p - 1, (p - 1) % 2, psT[(p - 1) % 2])
                transposes(GP - 1, 1, psT[1])
                pe.wait_ge(s_xtl, GP)
                pe.wait_ge(s_firstl, 1)
                half(0, 0, 0, psG, s_gate, range(KT))
                lora_in(0, 0)
                pe.wait_ge(s_moves, 1)
                half(1, 0, 0, psUp, s_up, range(KT // 2))
                select(0, 0, psU[1])
                select(0, 1, psU[0])
                half(1, 0, 0, psUp, s_up, range(KT // 2, KT))
                pe.wait_ge(s_um, 2)
                pe.wait_ge(s_gul, 1)
                half(0, 0, 0, psG, s_gate, [KT])
                half(1, 0, 0, psUp, s_up, [KT])
                gate(1, 1, 0)
                up(1, 1, 0)
                down(0, 0, first=True)
                inner(0, 0, 1, TOK)
                with pe.Fori(1, GROUPS - 1) as g:
                    turn(g, 2 * TOK - g * TOK)
                    inner(FT * g, 2 * TOK - g * TOK, g + 1, (g - 1) * TOK)
                turn(GROUPS - 1, TOK)
                inner(FT * (GROUPS - 1), TOK)
                down(T - 1, 1, final=True)
                pe.wait_ge(s_tab, 16 * (2 * KT + 1 + KT))
                table(KT)
                table(KT + 1)
                lora_down(GROUPS - 1)

        early.close()

        DUO = 2 * P
        DUOS = PAIRS // 2
        x2t = [sb(f"x2t{s}", [P, 2, KT, DUO], r32) for s in range(2)]
        u2 = sb("u2", [P, DUO])
        u2s = sb("u2s", [P, 2, DUO], r32)
        x3 = [[sb(f"x3_{s}_{q}", [P, FEAT]) for q in range(2)] for s in range(2)]
        x3s = [sb(f"x3s{q}", [P, 2, FEAT], r32) for q in range(2)]
        w3bd = [sb(f"w3bd{q}", [P, 2, P], r32) for q in range(2)]
        y = [sb(f"y{q}", [P, FEAT]) for q in range(2)]

        pT, pU, pL2, pL3 = bank[0:2], bank[6], (bank[7], bank[5]), bank[2:4]
        c_zero = sem("c_zero")
        c_out = [sem(f"c_out{q}") for q in range(2)]
        c_tr, c_xh, c_xl, c_u, c_um, c_uh, c_ul, c_l2, c_x3, c_x3h, c_x3l, c_w3h, c_w3l, c_l3, c_y = (sem(n) for n in
            ("c_tr", "c_xh", "c_xl", "c_u", "c_um", "c_uh", "c_ul", "c_l2", "c_x3", "c_x3h", "c_x3l", "c_w3h", "c_w3l",
             "c_l3", "c_y"))
        with nc.Block() as block:

            @block.sync
            def _(sp):
                def reload(d, s):
                    sp.wait_ge(c_tr, 2 * d + 2)
                    sp.dma_start(x2s[s][:, :, :], X1[:, ds(2 * d + 4, 2), :]).then_inc(c_x2[s], 16)

                def store(d):
                    for q in range(2):
                        sp.wait_ge(c_y, 2 * d + q + 1)
                        sp.dma_start(out_pairs[ds((2 * d + q) * P, P), :], y[q][:, :]).then_inc(c_out[q], 16)

                reload(0, 0)
                reload(1, 1)
                with sp.Fori(1, DUOS // 2 - 1) as i:
                    for s in range(2):
                        reload(2 * i + s, s)
                        store(2 * i + s - 2)
                for d in range(DUOS - 4, DUOS):
                    store(d)
                for q in range(2):
                    sp.wait_ge(c_out[q], 16 * DUOS)

            @block.scalar
            def _(act):
                def xt_high(d, s):
                    for q in range(2):
                        act.wait_ge(c_tr, 2 * d + q + 1)
                        if later(d, 2) and q == 0:
                            act.wait_ge(c_l2, 2 * d - 2)
                        nc.scalar.activation(x2t[s][:, 0, :, q * P:(q + 1) * P],
                                             pT[q][:, :].rearrange("p (k t) -> p k t", k=KT), ACT.Copy).then_inc(c_xh, 1)

                def u_high(d):
                    act.wait_ge(c_um, d + 1)
                    if later(d, 1):
                        act.wait_ge(c_l2, 2 * d)
                    nc.scalar.activation(u2s[:, 0, :], u2[:, :], ACT.Copy).then_inc(c_uh, 1)

                def x3_high(d, s):
                    for q in range(2):
                        act.wait_ge(c_x3, 2 * d + q + 1)
                        if later(d, 1):
                            act.wait_ge(c_l3, 2 * d + q - 1)
                        nc.scalar.activation(x3s[q][:, 0, :], x3[s][q][:, :], ACT.Copy).then_inc(c_x3h, 1)
                        for h in range(2):
                            rows = slice(h * POS, (h + 1) * POS)
                            last = nc.scalar.activation(w3bd[q][rows, 0, rows], w3raw[rows, ds(2 * d + q, 1), :], ACT.Copy)
                        last.then_inc(c_w3h, 1)

                act.wait_ge(c_zero, 2)
                xt_high(0, 0)
                xt_high(1, 1)
                u_high(0)

                def duos(i):
                    for s in range(2):
                        d = 2 * i + s
                        x3_high(d - 2, s)
                        xt_high(d, s)
                        u_high(d - 1)

                duos(1)
                with act.Fori(2, DUOS // 2) as i:
                    duos(i)
                x3_high(DUOS - 2, 0)
                u_high(DUOS - 1)
                x3_high(DUOS - 1, 1)

            @block.vector
            def _(dve):
                for q in range(2):
                    nc.vector.memset(w3bd[q][:, :, :].bitcast(f32), 0.0).then_inc(c_zero, 1)
                def xt_low(d, s):
                    for q in range(2):
                        dve.wait_ge(c_xh, 2 * d + q + 1)
                        nc.vector.tensor_tensor(x2t[s][:, 1, :, q * P:(q + 1) * P],
                                                pT[q][:, :].rearrange("p (k t) -> p k t", k=KT),
                                                x2t[s][:, 0, :, q * P:(q + 1) * P].bitcast(f32), ALU.subtract).then_inc(c_xl, 1)

                def u_mask(d):
                    dve.wait_ge(c_u, d + 1)
                    nc.vector.tensor_tensor(u2[:, :].rearrange("p (b t) -> p b t", t=POS),
                                            pU[:, 0:DUO].rearrange("p (b t) -> p b t", t=POS),
                                            mask2[:, ds(4 * d, 4)].unsqueeze(2).to_broadcast([P, 4, POS]),
                                            ALU.mult).then_inc(c_um, 1)
                    dve.wait_ge(c_uh, d + 1)
                    nc.vector.tensor_tensor(u2s[:, 1, :], u2[:, :], u2s[:, 0, :].bitcast(f32),
                                            ALU.subtract).then_inc(c_ul, 1)

                def x3_low(d, s, pairs=range(2)):
                    for q in pairs:
                        dve.wait_ge(c_x3h, 2 * d + q + 1)
                        nc.vector.tensor_tensor(x3s[q][:, 1, :], x3[s][q][:, :], x3s[q][:, 0, :].bitcast(f32),
                                                ALU.subtract).then_inc(c_x3l, 1)
                        dve.wait_ge(c_w3h, 2 * d + q + 1)
                        for h in range(2):
                            rows = slice(h * POS, (h + 1) * POS)
                            last = nc.vector.tensor_tensor(w3bd[q][rows, 1, rows],
                                                           w3raw[rows, ds(2 * d + q, 1), :].rearrange("p a d -> p (a d)"),
                                                           w3bd[q][rows, 0, rows].bitcast(f32), ALU.subtract)
                        last.then_inc(c_w3l, 1)

                def x3_sum(d, s, q):
                    dve.wait_ge(c_l2, 2 * d + q + 1)
                    nc.vector.tensor_tensor(x3[s][q][:, :], pL2[q][:, :],
                                            X1[:, ds(2 * d + q, 1), :].rearrange("p a t -> p (a t)"), ALU.add).then_inc(c_x3, 1)

                def y_sum(d, s, q):
                    dve.wait_ge(c_l3, 2 * d + q + 1)
                    if later(d, 1):
                        dve.wait_ge(c_out[q], 16 * d)
                    nc.vector.tensor_tensor(y[q][:, :], pL3[q][:, :], x3[s][q][:, :], ALU.add).then_inc(c_y, 1)

                xt_low(0, 0)
                xt_low(1, 1)
                for j in range(GP):
                    dst = X1[:, PAIRS - GP + j, :]
                    last = nc.vector.tensor_tensor(dst, psD[j][:, :], dst, ALU.add)
                last.then_inc(s_x2, 1)
                u_mask(0)
                x3_sum(0, 0, 0)
                x3_sum(0, 0, 1)
                def duos(i):
                    for s in range(2):
                        d = 2 * i + s
                        x3_low(d - 2, s)
                        xt_low(d, s)
                        u_mask(d - 1)
                        for q in range(2):
                            y_sum(d - 2, s, q)
                            x3_sum(d - 1, 1 - s, q)

                duos(1)
                with dve.Fori(2, DUOS // 2) as i:
                    duos(i)
                x3_low(DUOS - 2, 0)
                u_mask(DUOS - 1)
                x3_sum(DUOS - 1, 1, 0)
                for q in range(2):
                    y_sum(DUOS - 2, 0, q)
                x3_low(DUOS - 1, 1, [0])
                x3_sum(DUOS - 1, 1, 1)
                x3_low(DUOS - 1, 1, [1])
                for q in range(2):
                    y_sum(DUOS - 1, 1, q)

            @block.tensor
            def _(pe):
                def transposes(d, s, n):
                    pe.wait_ge(c_x2[s], 16 * (n + 1))
                    for q in range(2):
                        if later(d, 1):
                            pe.wait_ge(c_xl, 2 * d + q - 1)
                        for k in range(KT):
                            last = nc.tensor.transpose(pT[q][:, k * P:(k + 1) * P], x2s[s][:, q, k * P:(k + 1) * P], ident[:, :])
                        last.then_inc(c_tr, 1)

                def lora_in(d, s):
                    pe.wait_ge(c_xl, 2 * d + 2)
                    if later(d, 1):
                        pe.wait_ge(c_um, d)
                    for k in range(KT):
                        for n, (a, b) in enumerate(((0, 0), (0, 1), (1, 0))):
                            last = nc.tensor.matmul(pU[:, 0:DUO], A2T[:, a, k, :], x2t[s][:, b, k, :],
                                                    start=(k == 0 and n == 0), stop=(k == KT - 1 and n == 2))
                    last.then_inc(c_u, 1)

                def layer2(d, s, q):
                    if later(d, 1):
                        pe.wait_ge(c_x3, 2 * d + q - 1)
                    for k in range(KT):
                        for n, (a, b) in enumerate(((0, 0), (0, 1), (1, 0))):
                            nc.tensor.matmul(pL2[q][:, :], x2t[s][:, a, k, q * P:(q + 1) * P], W2T[:, b, k, :],
                                             start=(k == 0 and n == 0), stop=False)

                def lora_out(d, q):
                    pe.wait_ge(c_ul, d + 1)
                    for n, (a, b) in enumerate(((0, 0), (0, 1), (1, 0))):
                        last = nc.tensor.matmul(pL2[q][:, :], u2s[:, a, q * P:(q + 1) * P], B2T[:, b, :], start=False, stop=(n == 2))
                    last.then_inc(c_l2, 1)

                def layer3(d, q):
                    pe.wait_ge(c_x3l, 2 * d + q + 1)
                    pe.wait_ge(c_w3l, 2 * d + q + 1)
                    if later(d, 1):
                        pe.wait_ge(c_y, 2 * d + q - 1)
                    for n, (a, b) in enumerate(((0, 0), (0, 1), (1, 0))):
                        last = nc.tensor.matmul(pL3[q][:, :], w3bd[q][:, a, :], x3s[q][:, b, :], start=(n == 0), stop=(n == 2))
                    last.then_inc(c_l3, 1)

                transposes(0, 0, 0)
                transposes(1, 1, 0)
                lora_in(0, 0)
                layer2(0, 0, 0)
                pe.wait_ge(s_x2, GROUPS)
                layer2(0, 0, 1)
                for q in range(2):
                    lora_out(0, q)

                def duos(i):
                    for s in range(2):
                        d = 2 * i + s
                        transposes(d, s, i)
                        lora_in(d - 1, 1 - s)
                        for q in range(2):
                            layer2(d - 1, 1 - s, q)
                        for q in range(2):
                            layer3(d - 2, q)
                            lora_out(d - 1, q)

                duos(1)
                with pe.Fori(2, DUOS // 2) as i:
                    duos(i)
                lora_in(DUOS - 1, 1)
                layer2(DUOS - 1, 1, 0)
                lora_out(DUOS - 1, 0)
                for q in range(2):
                    layer3(DUOS - 2, q)
                layer2(DUOS - 1, 1, 1)
                lora_out(DUOS - 1, 1)
                for q in range(2):
                    layer3(DUOS - 1, q)


_INS = ['x', 'itok_B_0_7', 'fside_8xS_0', 'itok_B_0_6', 'itok_B_1_198', 'L0_cond_weights', 'L1_cond_Wg', 'L1_cond_Wu',
        'L1_cond_Wd', 'L1_cond_Ag', 'L1_cond_Bg', 'L1_cond_Au', 'L1_cond_Bu', 'L1_cond_Ad', 'L1_cond_Bd', 'L2_cond_W',
        'L2_cond_A', 'L2_cond_Bm', 'L2_cond_scalings', 'L3_cond_weights']
_OUTS = [((32, 64, 512), 'float32')]


def kernel(**inputs):
    import numpy as _np
    import concourse.bacc as _bacc
    from concourse import mybir as _mybir
    from concourse.bass_utils import run_bass_kernel_spmd as _run

    nc = _bacc.Bacc("TRN2", target_bir_lowering=False, num_devices=1, dynamic_dma_scratch_size=4096)
    arrays, args = {}, []
    for name in _INS:
        a = _np.ascontiguousarray(inputs[name])
        arrays[f"in_{name}_dram"] = a
        args.append(nc.dram_tensor(f"in_{name}_dram", a.shape, _mybir.dt.from_np(a.dtype), kind="ExternalInput").ap())
    for i, (shape, dtype) in enumerate(_OUTS):
        dt = _mybir.dt.from_np(_np.dtype(dtype))
        args.append(nc.dram_tensor(f"out_{i}_dram", shape, dt, kind="ExternalOutput").ap())
    conditioned_residual_stack(nc, *args)
    r = _run(nc, [arrays], core_ids=[0])
    return r.results[0]["out_0_dram"]
```
